# Optimizing a Trainium2 kernel written in Bass

```python
import numpy as np
import jax
import jax.numpy as jnp

def _softmax(x, axis=-1):
    return jax.nn.softmax(x, axis=axis)

def _gelu(x):
    return jax.nn.gelu(x, approximate=True)

def _silu(x):
    return jax.nn.silu(x)

def _sigmoid(x):
    return jax.nn.sigmoid(x)

def _layernorm(x, axis=-1, eps=1e-05):
    m = jnp.mean(x, axis=axis, keepdims=True)
    v = jnp.var(x, axis=axis, keepdims=True)
    return (x - m) / jnp.sqrt(v + eps)

def _scatter_add(tgt, idx, src, axis=0):
    return tgt.at[idx].add(src)

def _segment_sum(src, seg, n):
    return jax.ops.segment_sum(src, seg, n)
kernel_name = 'mk_gnn_ffn_d1_gnn_r8_3ebd99'

def setup_inputs(seed: int=0):
    np.random.seed(seed)
    _w = jnp.asarray

    def _rec_inputs():
        import jax
        import jax.numpy as jnp
        _gk = jax.random.key(seed)
        x = -0.0003713 + 1 * jax.random.normal(jax.random.fold_in(_gk, 1), (6250, 256), jnp.float32)
        _s = jax.random.randint(jax.random.fold_in(_gk, 2), (100000,), 0, 6250, jnp.int32)
        _d = jax.random.randint(jax.random.fold_in(_gk, 3), (100000,), 0, 6250, jnp.int32)
        _loop = jnp.arange(6250, dtype=jnp.int32)
        src = jnp.concatenate([_s, _d, _loop])
        dst = jnp.concatenate([_d, _s, _loop])
        _o = jnp.argsort(dst, stable=True)
        src = src[_o]
        dst = dst[_o]
        edge_weight = jax.random.uniform(jax.random.fold_in(_gk, 12), (206250,), jnp.float32, 0.0, 0.999998)
        return (x, src, dst, edge_weight)
    x, src, dst, edge_weight = _rec_inputs()

    def _L0_gnn_setup():
        import jax, jax.numpy as jnp
        import numpy as np
        N_NODES = 6250
        N_EDGES = 37500
        D = 256
        EPS = 1e-12

        def _gcn_layer(x, W, b, src, dst, norm, n_nodes):
            xt = x @ W
            msg = xt[src] * norm[:, None]
            agg = jax.ops.segment_sum(msg, dst, num_segments=n_nodes)
            return jax.nn.relu(agg + b)
        key = jax.random.key(seed)
        ks = jax.random.split(key, 10)
        h5_all = jax.random.normal(ks[0], (N_NODES, D), dtype=jnp.float32)
        edge_index = jax.random.randint(ks[1], (2, N_EDGES), 0, N_NODES, dtype=jnp.int64)
        edge_weight = jax.random.uniform(ks[2], (N_EDGES,), dtype=jnp.float32)
        s = 1.0 / np.sqrt(D)
        W6 = jax.random.normal(ks[3], (D, D), dtype=jnp.float32) * s
        b6 = jnp.zeros((D,), dtype=jnp.float32)
        W7 = jax.random.normal(ks[4], (D, D), dtype=jnp.float32) * s
        b7 = jnp.zeros((D,), dtype=jnp.float32)
        Wp = jax.random.normal(ks[5], (D, D), dtype=jnp.float32) * s
        bp = jnp.zeros((D,), dtype=jnp.float32)
        return {'h5_all': h5_all, 'edge_index': edge_index, 'edge_weight': edge_weight, 'W6': W6, 'b6': b6, 'W7': W7, 'b7': b7, 'Wp': Wp, 'bp': bp}
    _L0_gnn_all = _L0_gnn_setup()
    _L0_gnn_in = {k: v for k, v in _L0_gnn_all.items() if k in ('W6', 'b6', 'W7', 'b7', 'Wp', 'bp')}
    del _L0_gnn_all

    def _L0_ffn_setup():
        import jax, jax.numpy as jnp
        import numpy as np
        E = 8
        K = 2
        D = 256
        H = 512
        DOUT = 256
        EPS = 1e-05
        key = jax.random.key(seed)
        ks = jax.random.split(key, 9)
        s = 0.02
        return {'x': jax.random.normal(ks[0], (4, 1024, D), jnp.float32), 'gamma': 1.0 + 0.05 * jax.random.normal(ks[1], (D,), jnp.float32), 'beta': 0.05 * jax.random.normal(ks[2], (D,), jnp.float32), 'Wr': 0.01 * jax.random.normal(ks[3], (D, E), jnp.float32), 'br': jnp.zeros((E,), jnp.float32), 'W1': s * jax.random.normal(ks[4], (E, D, H), jnp.float32), 'b1': s * jax.random.normal(ks[5], (E, H), jnp.float32), 'W2': s * jax.random.normal(ks[6], (E, H, DOUT), jnp.float32), 'b2': s * jax.random.normal(ks[7], (E, DOUT), jnp.float32)}
    _L0_ffn_all = _L0_ffn_setup()
    _L0_ffn_in = {k: v for k, v in _L0_ffn_all.items() if k in ('gamma', 'beta', 'Wr', 'br', 'W1', 'b1', 'W2', 'b2')}
    del _L0_ffn_all
    return {'x': x, 'src': src, 'dst': dst, 'edge_weight': edge_weight, 'L0_gnn_W6': _L0_gnn_in['W6'], 'L0_gnn_b6': _L0_gnn_in['b6'], 'L0_gnn_W7': _L0_gnn_in['W7'], 'L0_gnn_b7': _L0_gnn_in['b7'], 'L0_gnn_Wp': _L0_gnn_in['Wp'], 'L0_gnn_bp': _L0_gnn_in['bp'], 'L0_ffn_gamma': _L0_ffn_in['gamma'], 'L0_ffn_beta': _L0_ffn_in['beta'], 'L0_ffn_Wr': _L0_ffn_in['Wr'], 'L0_ffn_br': _L0_ffn_in['br'], 'L0_ffn_W1': _L0_ffn_in['W1'], 'L0_ffn_b1': _L0_ffn_in['b1'], 'L0_ffn_W2': _L0_ffn_in['W2'], 'L0_ffn_b2': _L0_ffn_in['b2']}

def reference(x, src, dst, edge_weight, L0_gnn_W6, L0_gnn_b6, L0_gnn_W7, L0_gnn_b7, L0_gnn_Wp, L0_gnn_bp, L0_ffn_gamma, L0_ffn_beta, L0_ffn_Wr, L0_ffn_br, L0_ffn_W1, L0_ffn_b1, L0_ffn_W2, L0_ffn_b2):
    import jax
    import jax.numpy as jnp

    def _L0_gnn_ref(h5_all, edge_index, edge_weight, W6, b6, W7, b7, Wp, bp):
        import jax, jax.numpy as jnp
        import numpy as np
        N_NODES = 6250
        N_EDGES = 37500
        D = 256
        EPS = 1e-12

        def _gcn_layer(x, W, b, src, dst, norm, n_nodes):
            xt = x @ W
            msg = xt[src] * norm[:, None]
            agg = jax.ops.segment_sum(msg, dst, num_segments=n_nodes)
            return jax.nn.relu(agg + b)
        src, dst = (edge_index[0], edge_index[1])
        deg_out = jax.ops.segment_sum(edge_weight, src, num_segments=N_NODES)
        deg_in = jax.ops.segment_sum(edge_weight, dst, num_segments=N_NODES)
        norm = edge_weight * jax.lax.rsqrt(deg_out[src] * deg_in[dst] + EPS)
        h6 = _gcn_layer(h5_all, W6, b6, src, dst, norm, N_NODES)
        h7 = _gcn_layer(h6, W7, b7, src, dst, norm, N_NODES)
        out = h7 @ Wp + bp
        return out

    def _L0_ffn_ref(x, gamma, beta, Wr, br, W1, b1, W2, b2):
        import jax, jax.numpy as jnp
        import numpy as np
        E = 8
        K = 2
        D = 256
        H = 512
        DOUT = 256
        EPS = 1e-05
        mu = jnp.mean(x, axis=-1, keepdims=True)
        var = jnp.mean(jnp.square(x - mu), axis=-1, keepdims=True)
        xn = (x - mu) * jax.lax.rsqrt(var + EPS) * gamma + beta
        logits = jnp.einsum('bsd,de->bse', xn, Wr) + br
        top_vals, top_idx = jax.lax.top_k(logits, K)
        w = jax.nn.softmax(top_vals, axis=-1)
        w_full = jnp.einsum('bsk,bske->bse', w, jax.nn.one_hot(top_idx, E, dtype=w.dtype))
        y = jnp.zeros(x.shape[:-1] + (DOUT,), x.dtype)
        for e in range(E):
            h = jax.nn.gelu(jnp.einsum('bsd,dh->bsh', xn, W1[e]) + b1[e], approximate=False)
            y_e = jnp.einsum('bsh,hd->bsd', h, W2[e]) + b2[e]
            y = y + y_e * w_full[..., e, None]
        return y
    edge_index = jnp.stack([src, dst])
    x = x + _L0_gnn_ref(_layernorm(x, axis=-1), edge_index, edge_weight, L0_gnn_W6, L0_gnn_b6, L0_gnn_W7, L0_gnn_b7, L0_gnn_Wp, L0_gnn_bp)
    x = x + _L0_ffn_ref(_layernorm(x, axis=-1)[None], L0_ffn_gamma, L0_ffn_beta, L0_ffn_Wr, L0_ffn_br, L0_ffn_W1, L0_ffn_b1, L0_ffn_W2, L0_ffn_b2)[0]
    return x

_drawn_inputs = setup_inputs


def setup_inputs(seed=0):
    import zlib

    import numpy as np

    out = dict(_drawn_inputs(seed))
    spreads = {'L0_gnn_b6': (0.0, 0.1),
     'L0_gnn_b7': (0.0, 0.1),
     'L0_gnn_bp': (0.0, 0.1),
     'L0_ffn_br': (0.0, 0.1)}
    factors = {'edge_weight': 4.455,
     'L0_gnn_W6': 2.701,
     'L0_ffn_gamma': 5.632,
     'L0_ffn_beta': 4.849,
     'L0_ffn_b1': 8.0,
     'L0_ffn_b2': 4.253}
    for name, (base, spread) in spreads.items():
        noise = np.random.default_rng([zlib.crc32(name.encode()), seed]).standard_normal(out[name].shape)
        drawn = base * np.exp(spread * noise) if base else spread * noise
        out[name] = jnp.asarray(drawn.astype(out[name].dtype))
    for name, factor in factors.items():
        out[name] = (out[name] * factor).astype(out[name].dtype)
    return out
```

```python
from contextlib import ExitStack

import concourse.bass as bass
from concourse import mybir

F32 = mybir.dt.float32
I32 = mybir.dt.int32
U32 = mybir.dt.uint32
ALU = mybir.AluOpType
ACT = mybir.ActivationFunctionType
AX_X = mybir.AxisListType.X
RMAX = bass.bass_isa.ReduceOp.max

P = 128
TG = 8
WIN = 64
GPI = 4
LAG_PREP = 3
LAG_EXP = 4
RSQRT_MAGIC = 0x5F3759DF


def ceil_div(a, b):
    return -(-a // b)


class Links:

    def __init__(self, eng, sem):
        self.eng, self.sem, self.base, self.n = eng, sem, 0, 0

    def at(self, base):
        self.base, self.n = base, 0
        return self

    def __call__(self, ins, wait=None):
        self.n += 1
        ins.then_inc(self.sem, 1)
        if wait:
            wait(self.eng, self.sem, self.base + self.n)
        else:
            self.eng.wait_ge(self.sem, self.base + self.n)


def gnn_moe_kernel(nc, A):
    x, src, dst, ew = A["x"], A["src"], A["dst"], A["edge_weight"]
    out = A["out"]
    N, D = A["n_nodes"], x.shape[1]
    E8 = src.shape[1]
    NG = A["n_groups"]
    NE = A["n_experts"]
    H = A["hidden"]
    KD = D // P
    HC = H // P
    NIT = E8 // (TG * GPI)
    FULL, REM = NG // GPI, NG % GPI
    NB = ceil_div(N, P)
    NPASS = NB * P // WIN
    AW = NB * P + WIN
    ROW = D + 1
    LAST_ROWS = N - (NB - 1) * P
    assert KD == 2 and D == 256 and NE == 8 and HC == 4 and FULL > LAG_EXP and NB > LAG_EXP
    assert (NIT - 1) * GPI < NG <= NIT * GPI and NB < NIT
    EXPERT_W = NE * KD * H

    with ExitStack() as ctx:
        def sb(name, shape, dt=F32):
            return ctx.enter_context(nc.sbuf_tensor(name, shape, dt))

        def sem(name):
            return ctx.enter_context(nc.semaphore(name))

        def sems(name, n):
            return [sem(f"{name}{i}") for i in range(n)]

        table = [nc.dram_tensor(f"table{i}", (NB * P, ROW), F32, kind="Internal").ap() for i in range(2)]

        w_sb = sb("w_sb", [P, E8])
        dst_f = sb("dst_f", [P, E8])
        agg = sb("agg", [P, KD, AW])
        w1_di = sb("w1_di", [P, max(EXPERT_W, AW)])
        w2_src = sb("w2_src", [P, max(NE * HC * D, 4 * E8)])
        gat = sb("gat", [P, GPI, TG, ROW])
        idx = sb("idx", [P, GPI, TG], I32)
        s_mat = sb("s_mat", [P, GPI, TG, WIN])
        oh_win = sb("oh_win", [P, 2, TG, WIN])
        di_bc = w1_di[:, 0:AW]
        w1_sb = w1_di[:, 0:EXPERT_W].rearrange("p (e k h) -> p e k h", e=NE, k=KD)
        w2_sb = w2_src[:, 0:NE * HC * D].rearrange("p (e c n) -> p e c n", e=NE, c=HC)
        src_i = w2_src[:, 0:E8].bitcast(I32)
        dst_i = w2_src[:, E8:2 * E8].bitcast(I32)
        src_hi_i = w2_src[:, 2 * E8:3 * E8].bitcast(I32)
        src_lo_i = w2_src[:, 3 * E8:4 * E8].bitcast(I32)
        src_hi = w2_src[:, 0:E8]
        src_lo = w2_src[:, E8:2 * E8]
        gflat = gat[:].rearrange("p a b c -> p (a b c)")
        oh_lo = gflat[:, 0:2 * TG * P].rearrange("p (a t n) -> p a t n", a=2, t=TG)
        oh_hi = gflat[:, 2 * TG * P:2 * TG * (P + NB)].rearrange("p (a t n) -> p a t n", a=2, t=TG)
        o2 = 2 * TG * (P + NB)
        whi = gflat[:, o2:o2 + 2 * TG * NB].rearrange("p (a t n) -> p a t n", a=2, t=TG)
        wst = sb("wst", [P, 2, TG])

        iota_i = sb("iota_i", [P, P], I32)
        iota_f = sb("iota_f", [P, P])
        row_i = sb("row_i", [P, 1], I32)
        row_f = sb("row_f", [P, 1])
        ident = sb("ident", [P, P])
        need_i = sb("need_i", [P, NIT * GPI], I32)
        need_f = sb("need_f", [P, NIT * GPI])
        ends = sb("ends", [P, 2, NIT * GPI])
        ends_all = sb("ends_all", [P, 2, NIT * GPI])
        base_f = sb("base_f", [P, NIT * GPI])
        base_i = sb("base_i", [P, NIT * GPI], I32)
        viol = sb("viol", [P, 2, NIT * GPI])
        bad_f = sb("bad_f", [P, 2])
        bad_i = sb("bad_i", [P, 1], I32)
        wbase = sb("wbase", [P, 1])
        eps = sb("eps", [P, 2])
        do_col = sb("do_col", [P, NB])
        di_col = sb("di_col", [P, NB])

        w6 = sb("w6", [P, KD, D])
        w7 = sb("w7", [P, KD, D])
        wp = sb("wp", [P, KD, D])
        wr = sb("wr", [P, KD, NE])
        cols = sb("cols", [P, 4 * KD + NE * HC])
        b6c, b7c, gac, bec = (cols[:, KD * i:KD * (i + 1)] for i in range(4))
        b1c = cols[:, 4 * KD:]
        b2s = sb("b2s", [NE, D])
        br_bc = sb("br_bc", [P, NE])
        bp_bc = sb("bp_bc", [P, D])

        xin = sb("xin", [P, D])
        st6 = sb("st6", [P, 6])
        mv = sb("mv", [P, 2])
        sd1 = sb("sd1", [P, 1])
        rstd = sb("rstd", [P, 1])
        xn = sb("xn", [P, D])
        xT = sb("xT", [P, KD, P])
        feat = sb("feat", [P, D])
        hT = sb("hT", [P, KD, P])
        zero = sb("zero", [P, D])

        rel = sb("rel", [P, TG])
        di8 = sb("di8", [P, TG])
        t8 = sb("t8", [P, TG])
        sd8 = sb("sd8", [P, TG])
        r8 = sb("r8", [P, TG])
        nrm8 = sb("nrm8", [P, TG])

        x1 = sb("x1", [P, D])
        xs = sb("xs", [P, D])
        rv = sb("rv", [P, 8])
        rvi = sb("rvi", [P, 1], I32)
        lg = sb("lg", [P, NE])
        mx8 = sb("mx8", [P, 8])
        mi8 = sb("mi8", [P, 8], U32)
        mif = sb("mif", [P, 2])
        dlt = sb("dlt", [P, 2])
        wtop = sb("wtop", [P, 2])
        wsel = sb("wsel", [P, 2, NE])
        wf = sb("wf", [P, P])
        wT = sb("wT", [P, P])
        hs = sb("hs", [P, 2, HC, P])
        yacc = sb("yacc", [P, D])

        bank = [ctx.enter_context(nc.psum_tensor(f"bank{i}", [P, 512], F32)) for i in range(8)]
        ps_seg = [bank[i][:, 0:KD * WIN].rearrange("p (k n) -> p k n", k=KD) for i in range(2)]
        ps_win = [bank[i][:, 0:WIN] for i in range(2)]
        ps_do = bank[2][:, 0:NB]
        ps_xT = bank[3][:, 0:D].rearrange("p (k n) -> p k n", k=KD)
        ps_feat = bank[4][:, 0:D]
        ps_h = [bank[2 + i][:, :].rearrange("p (c n) -> p c n", c=HC) for i in range(2)]
        ps_y = [bank[4 + i][:, 0:D] for i in range(2)]
        ps_proj = bank[6][:, 0:D]
        ps_zT = bank[6][:, D:2 * D].rearrange("p (k n) -> p k n", k=KD)
        ps_lg = bank[7][:, 0:NE]
        ps_wT = bank[7][:, P:2 * P]
        ps_b2 = bank[7][:, D:2 * D]

        edges_in, w_in, consts_in = sem("edges_in"), sem("w_in"), sem("consts_in")
        iota_made, dve_setup = sem("iota_made"), sem("dve_setup")
        ends_made, ends_shared = sem("ends_made"), sem("ends_shared")
        setup_done = sem("setup_done")
        lo_ready, hi_ready, win_ready = sem("lo_ready"), sem("hi_ready"), sem("win_ready")
        whi_ready, wst_ready = sem("whi_ready"), sem("wst_ready")
        deg_mm, di_added = sems("deg_mm", 2), sems("di_added", 2)
        win_mm, wwst_ready = sems("win_mm", 2), sem("wwst_ready")
        deg_links, do_closed, do_made, do_in_tables = sem("deg_links"), sem("do_closed"), sem("do_made"), sem("do_in_tables")
        x_in, f_mv, f_std, f_norm = sem("x_in"), sem("f_mv"), sem("f_std"), sem("f_norm")
        f_links, f_T, f_xT, f_mm, f_feat, f_stored = (sem(n) for n in ("f_links", "f_T", "f_xT", "f_mm", "f_feat", "f_stored"))
        idx_in = [sems(f"idx_in{L}_", GPI) for L in range(2)]
        gathered = [sems(f"gathered{L}_", GPI) for L in range(2)]
        seg_done = [sems(f"seg_done{L}_", GPI) for L in range(2)]
        seg_links = sems("seg_links", 2)
        prod_ready, root_ready = sems("prod_ready", 2), sems("root_ready", 2)
        s_ready = sems("s_ready", 2)
        added = [sems(f"added{L}_", 2) for L in range(2)]
        window_moved = sems("window_moved", 3)
        p_h, p_zeroed, p_mm, p_out, p_stored = (sem(n) for n in ("p_h", "p_zeroed", "p_mm", "p_out", "p_stored"))
        w1_in, w2_in, xb_in = sem("w1_in"), sem("w2_in"), sem("xb_in")
        h7_ready, proj_mm, ln_links, x1_ready, u_ready, z_ready, zT_mm, zT_ready = (
            sem(n) for n in ("h7_ready", "proj_mm", "ln_links", "x1_ready", "u_ready", "z_ready", "zT_mm", "zT_ready"))
        lg_mm, router_links, delta_ready, tanh_ready, wf_ready, wT_mm, wT_ready, b2_mm, b2_added = (
            sem(n) for n in ("lg_mm", "router_links", "delta_ready", "tanh_ready", "wf_ready", "wT_mm", "wT_ready",
                             "b2_mm", "b2_added"))
        h_mm, gelu_done, y_mm, y_added = (sems(n, 2) for n in ("h_mm", "gelu_done", "y_mm", "y_added"))
        out_stored = sem("out_stored")

        N_CONSTS = 12
        SETUP_DONE = 3

        block = ctx.enter_context(nc.Block())

        def bc_mid(ap, n):
            return ap.unsqueeze(1).broadcast_to([P, n, ap.shape[-1]])

        def bc_in(ap, n):
            return ap.unsqueeze(2).broadcast_to([P, ap.shape[-1], n])

        def tiles(ap, it, s):
            return ap[:, bass.ds(it * (GPI * TG) + s * TG, TG)]

        def add_before(s, n):
            return (1, n * 2 + s // 2) if s % 2 == 0 else (0, n * 2 + (s + 1) // 2)

        def wait_apart(eng, sem_, value):
            if not isinstance(value, int):
                eng.compute_val(value)
            eng.wait_ge(setup_done, SETUP_DONE)
            eng.wait_ge(sem_, value)

        def flag(eng):
            eng.wait_ge(setup_done, SETUP_DONE)
            return eng.value_load(bad_i[0:1, 0:1], min_val=0, max_val=1)

        def all_windows(eng, f, before_pass=None):
            with eng.Fori(0, NPASS) as w:
                if before_pass:
                    before_pass(w)
                with eng.Fori(0, NIT) as it:
                    f(it, w * NIT + it, w)

        SLOW_ITS = NPASS * NIT

        @block.sync
        def _(sp):
            sp.dma_start(src_i, src).then_inc(edges_in, 16)
            sp.dma_start(dst_i, dst).then_inc(edges_in, 16)
            sp.dma_start(w_sb[:, :], ew).then_inc(w_in, 16)
            for t, a in ((w6[:], A["W6"]), (w7[:], A["W7"]), (wp[:], A["Wp"]), (wr[:], A["Wr"])):
                sp.dma_start(t, a.rearrange("(k p) n -> p k n", p=P)).then_inc(consts_in, 16)
            for t, a in ((b6c, A["b6"]), (b7c, A["b7"]), (gac, A["gamma"]), (bec, A["beta"]), (b1c, A["b1"]),
                         (b2s[:, :], A["b2"]), (br_bc[:, :], A["br"].broadcast_to([P, NE])),
                         (bp_bc[:, :], A["bp"].broadcast_to([P, D]))):
                sp.dma_start(t, a).then_inc(consts_in, 16)

            def feature_block(it):
                sp.wait_ge(f_norm, it)
                sp.dma_start(xin[:, :], x[bass.ds(it * P, P), :]).then_inc(x_in, 16)
                sp.wait_ge(f_feat, it + 1)
                sp.dma_start(table[0][bass.ds(it * P, P), 0:D], feat[:, :]).then_inc(f_stored, 16)

            def features():
                with sp.Fori(0, NB) as it:
                    feature_block(it)
                sp.wait_ge(lo_ready, NIT * GPI)
                sp.wait_ge(hi_ready, NIT * GPI)
                sp.dma_start(w2_sb, A["W2"].rearrange("p (e c n) -> p e c n", e=NE, c=HC)).then_inc(w2_in, 16)
                sp.wait_ge(do_made, 1)
                for t in table:
                    sp.dma_start(t[:, D:ROW].rearrange("(b p) a -> p (b a)", p=P), do_col[:, :],
                                 allow_slow_non_contiguous=True).then_inc(do_in_tables, 16)

            def indices(L, it, n, groups=GPI):
                for s in range(groups):
                    sp.wait_ge(gathered[L][s], n * (16 * TG))
                    sp.dma_start(idx[:, s, :], tiles(src, it, s)).then_inc(idx_in[L][s], 16)

            def store_table(b):
                sp.wait_ge(p_out, b + 1)
                sp.dma_start(table[1][bass.ds(b * P, P), 0:D], feat[:, :]).then_inc(p_stored, 16)

            def load_x(b):
                sp.wait_ge(x1_ready, b)
                sp.dma_start(xin[:, :], x[bass.ds(b * P, P), :]).then_inc(xb_in, 16)

            def store_out(b, rows=P):
                sp.wait_ge(y_added[1], b * (NE // 2) + NE // 2)
                sp.dma_start(out[bass.ds(b * P, rows), :], yacc[0:rows, :]).then_inc(out_stored, 16)

            def load_w1():
                sp.dma_start(w1_sb, A["W1"].rearrange("p (e k h) -> p e k h", e=NE, k=KD)).then_inc(w1_in, 16)

            bad = flag(sp)
            features()
            with sp.If(bad < 1):
                with sp.Fori(0, LAG_PREP) as it:
                    indices(0, it, it)
                with sp.Fori(LAG_PREP, FULL) as it:
                    indices(0, it, it)
                    store_table(it - LAG_PREP)
                indices(0, FULL, FULL, REM)
                for b in range(FULL - LAG_PREP, NB):
                    store_table(b)
                sp.wait_ge(s_ready[0], NG)
                load_w1()
                with sp.Fori(0, LAG_PREP) as it:
                    indices(1, it, it)
                indices(1, LAG_PREP, LAG_PREP)
                load_x(0)
                with sp.Fori(LAG_EXP, FULL) as it:
                    indices(1, it, it)
                    load_x(it - LAG_PREP)
                    store_out(it - LAG_EXP)
                indices(1, FULL, FULL, REM)
                for it in range(FULL, NB + LAG_EXP):
                    if it - LAG_PREP < NB:
                        load_x(it - LAG_PREP)
                    b = it - LAG_EXP
                    store_out(b, P if b < NB - 1 else LAST_ROWS)
            with sp.Else():
                all_windows(sp, lambda it, n, w: indices(0, it, n))
                with sp.Fori(0, NB) as b:
                    store_table(b)
                all_windows(sp, lambda it, n, w: indices(1, it, n))
                sp.wait_ge(s_ready[1], SLOW_ITS * GPI)
                load_w1()
                with sp.Fori(0, NB - 1) as b:
                    load_x(b)
                    store_out(b)
                load_x(NB - 1)
                store_out(NB - 1, LAST_ROWS)
            sp.wait_ge(out_stored, 16 * NB)

        @block.gpsimd
        def _(pool):
            pool.iota(iota_i[:, :], pattern=[[1, P]], base=0, channel_multiplier=0).then_inc(iota_made, 1)
            pool.iota(row_i[:, :], pattern=[[0, 1]], base=0, channel_multiplier=1).then_inc(iota_made, 1)
            pool.iota(need_i[:, :], pattern=[[P, NIT], [0, GPI]], base=-(LAG_PREP - 1) * P,
                      channel_multiplier=0).then_inc(iota_made, 1)
            pool.wait_ge(ends_made, 2)
            pool.partition_all_reduce(ends_all[:].rearrange("p a g -> p (a g)"), ends[:].rearrange("p a g -> p (a g)"),
                                      P, RMAX).then_inc(ends_shared, 1)

            def gathers(L, n, groups=GPI):
                for s in range(groups):
                    wait_apart(pool, idx_in[L][s], n * 16 + 16)
                    pool.wait_ge(seg_done[L][s], n)
                    for j in range(TG):
                        pool.indirect_dma_start(gat[:, s, j, :], None, table[L],
                                                bass.IndirectOffsetOnAxis(ap=idx[:, s, j:j + 1], axis=0)
                                                ).then_inc(gathered[L][s], 16)

            def table_ready(L):
                pool.wait_ge(do_in_tables, 32)
                pool.wait_ge(*((f_stored, 16 * NB) if L == 0 else (p_stored, 16 * NB)))

            bad = flag(pool)
            with pool.If(bad < 1):
                for L in range(2):
                    table_ready(L)
                    with pool.Fori(0, FULL) as it:
                        gathers(L, it)
                    gathers(L, FULL, REM)
            with pool.Else():
                for L in range(2):
                    table_ready(L)
                    all_windows(pool, lambda it, n, w: gathers(L, n))

        @block.vector
        def _(dve):
            step = Links(dve, dve_setup)
            dve.memset(zero[:, :], 0.0)
            dve.memset(wf[:, :], 0.0)
            dve.memset(eps[:, 0:1], 1e-12)
            dve.memset(eps[:, 1:2], 1e-5)
            dve.memset(di_bc, 0.0)
            dve.memset(agg[:].rearrange("p k n -> p (k n)"), 0.0)
            dve.wait_ge(edges_in, 32)
            step(dve.tensor_copy(dst_f[:, :], dst_i))
            step(dve.tensor_single_scalar(src_hi_i, src_i, 7, op=ALU.logical_shift_right))
            step(dve.tensor_single_scalar(src_lo_i, src_i, P - 1, op=ALU.bitwise_and))
            dve.tensor_copy(src_hi, src_hi_i)
            dve.tensor_copy(src_lo, src_lo_i)
            by_group = dst_f[:, :].rearrange("p (g t) -> p g t", t=TG)
            dve.tensor_reduce(ends[:, 0, :], by_group, AX_X, ALU.max).then_inc(ends_made, 1)
            dve.tensor_reduce(ends[:, 1, :], by_group, AX_X, ALU.min, negate=True).then_inc(ends_made, 1)
            dve.wait_ge(iota_made, 3)
            dve.tensor_copy(iota_f[:, :], iota_i[:, :])
            dve.tensor_copy(row_f[:, :], row_i[:, :])
            step(dve.tensor_copy(need_f[:, :], need_i[:, :]))
            step(dve.tensor_scalar(ident[:, :], iota_f[:, :], row_f[:, 0:1], None, ALU.is_equal))
            dve.wait_ge(ends_shared, 1)
            step(dve.tensor_scalar(base_f[:, :], ends_all[:, 1, :], -1.0, None, ALU.mult))
            dve.tensor_copy(base_i[:, :], base_f[:, :]).then_inc(setup_done, 1)
            step(dve.tensor_tensor(viol[:, 0, :], ends_all[:, 0, :], base_f[:, :], ALU.subtract))
            step(dve.tensor_scalar(viol[:, 0, :], viol[:, 0, :], float(WIN), None, ALU.is_ge))
            step(dve.tensor_tensor(viol[:, 1, :], base_f[:, :], need_f[:, :], ALU.is_lt))
            step(dve.tensor_reduce(bad_f[:, :], viol[:, :, 0:NG], AX_X, ALU.max))
            step(dve.tensor_tensor(bad_f[:, 0:1], bad_f[:, 0:1], bad_f[:, 1:2], ALU.max))
            dve.tensor_copy(bad_i[:, :], bad_f[:, 0:1]).then_inc(setup_done, 1)
            dve.tensor_copy(bad_f[:, 1:2], bad_f[:, 0:1]).then_inc(setup_done, 1)

            deg = Links(dve, deg_links)
            feats = Links(dve, f_links)

            def one_hots(it, s):
                dve.wait_ge(deg_mm[s % 2], it * 2 + s // 2)
                dve.tensor_tensor(oh_lo[:, s % 2], bc_mid(iota_f[:, :], TG), bc_in(tiles(src_lo, it, s), P),
                                  ALU.is_equal).then_inc(lo_ready, 1)
                dve.tensor_tensor(oh_hi[:, s % 2], bc_mid(iota_f[:, 0:NB], TG), bc_in(tiles(src_hi, it, s), NB),
                                  ALU.is_equal).then_inc(hi_ready, 1)

            def window_one_hot(it, s, n, base_col):
                deg.at(n * GPI + s)
                deg(dve.tensor_scalar(rel[:, :], tiles(dst_f, it, s), base_col, None, ALU.subtract))
                dve.wait_ge(win_mm[s % 2], n * 2 + s // 2)
                dve.tensor_tensor(oh_win[:, s % 2], bc_mid(iota_f[:, 0:WIN], TG), bc_in(rel[:, :], WIN),
                                  ALU.is_equal).then_inc(win_ready, 1)
                dve.wait_ge(win_ready, n * GPI + s + 1)

            def add_degrees(s, n, base):
                dve.wait_ge(win_mm[s % 2], n * 2 + s // 2 + 1)
                par, k = add_before(s, n)
                dve.wait_ge(di_added[par], k)
                win = di_bc[:, bass.ds(base, WIN)]
                dve.tensor_tensor(win, win, ps_win[s % 2], ALU.add).then_inc(di_added[s % 2], 1)

            def group_base(it, s):
                return dve.value_load(base_i[0:1, bass.ds(it * GPI + s, 1)], min_val=0, max_val=N - 1)

            def base_col(it, s):
                return base_f[:, bass.ds(it * GPI + s, 1)]

            def feature_norm(it, stage):
                if stage == 0:
                    feats.at(it * 2)
                    dve.wait_ge(x_in, it * 16 + 16)
                    feats(dve.bn_stats(st6[:, :], xin[:, :]), wait_apart)
                    dve.wait_ge(f_norm, it)
                    dve.bn_aggr(mv[:, :], st6[:, :]).then_inc(f_mv, 1)
                    dve.wait_ge(f_mv, it + 1)
                else:
                    feats.at(it * 2 + 1)
                    dve.wait_ge(f_std, it + 1)
                    feats(dve.reciprocal(rstd[:, :], sd1[:, :]))
                    dve.wait_ge(f_T, it)
                    dve.tensor_scalar(xn[:, :], xin[:, :], mv[:, 0:1], rstd[:, 0:1], ALU.subtract,
                                      ALU.mult).then_inc(f_norm, 1)

            def degree_iteration(it, fast, features):
                for s in range(GPI):
                    one_hots(it, s)
                    if fast:
                        window_one_hot(it, s, it, base_col(it, s))
                        if s > 0:
                            add_degrees(s - 1, it, group_base(it, s - 1))
                    if features and s == 0:
                        feature_norm(it, 0)
                    if features and s == 2:
                        feature_norm(it, 1)
                if fast:
                    add_degrees(GPI - 1, it, group_base(it, GPI - 1))

            def degrees(fast):
                with dve.Fori(0, NB) as it:
                    degree_iteration(it, fast, True)
                with dve.Fori(NB, NIT) as it:
                    degree_iteration(it, fast, False)
                dve.wait_ge(do_closed, 1)
                dve.tensor_copy(do_col[:, :], ps_do).then_inc(do_made, 1)

            seg = [Links(dve, seg_links[L]) for L in range(2)]

            def scatter_matrix(L, it, s, n, col, with_norms, norms, base=None):
                k = 6 if with_norms else 2
                link = seg[L].at((n * GPI + s) * k)
                oh = oh_win[:, 0]
                dve.wait_ge(s_ready[L], n * GPI + s)
                link(dve.tensor_scalar(rel[:, :], tiles(dst_f, it, s), col, None, ALU.subtract))
                link(dve.tensor_tensor(oh, bc_mid(iota_f[:, 0:WIN], TG), bc_in(rel[:, :], WIN), ALU.is_equal))
                if with_norms:
                    win = di_bc[:, bass.ds(base, WIN)]
                    link(dve.tensor_tensor(oh_win[:, 1], oh, bc_mid(win, TG), ALU.mult))
                    link(dve.tensor_reduce(di8[:, :], oh_win[:, 1], AX_X, ALU.add))
                    dve.wait_ge(gathered[L][s], n * (16 * TG) + 16 * TG)
                    dve.tensor_tensor(t8[:, :], di8[:, :], gat[:, s, :, D], ALU.mult).then_inc(prod_ready[L], 1)
                    dve.wait_ge(root_ready[L], n * GPI + s + 1)
                    link(dve.reciprocal(r8[:, :], sd8[:, :]))
                    link(dve.tensor_tensor(norms, r8[:, :], tiles(w_sb, it, s), ALU.mult))
                dve.wait_ge(seg_done[L][s], n)
                dve.tensor_tensor(s_mat[:, s], oh, bc_in(norms, WIN), ALU.mult).then_inc(s_ready[L], 1)

            def add_sums(L, s, n, base):
                dve.wait_ge(seg_done[L][s], n + 1)
                par, k = add_before(s, n)
                dve.wait_ge(added[L][par], k)
                win = agg[:, :, bass.ds(base, WIN)]
                dve.tensor_tensor(win, win, ps_seg[s % 2], ALU.add).then_inc(added[L][s % 2], 1)

            RSQRT_STEPS = 3 + 3 * 4
            LN_STEPS = 1 + 2 * (2 + RSQRT_STEPS)
            ln = Links(dve, ln_links)

            def rsqrt_of(var):
                v, y, a, b = (rv[:, i:i + 1] for i in range(4))
                ln(dve.tensor_scalar(v, var, 1e-5, None, ALU.add))
                ln(dve.tensor_single_scalar(rvi[:, :], v.bitcast(I32), 1, op=ALU.logical_shift_right))
                ln(dve.tensor_scalar(y.bitcast(I32), rvi[:, :], -1.0, float(RSQRT_MAGIC), ALU.mult, ALU.add))
                for _ in range(4):
                    ln(dve.tensor_tensor(a, y, y, ALU.mult))
                    ln(dve.tensor_scalar(b, a, v, -0.5, ALU.mult, ALU.mult))
                    ln(dve.scalar_tensor_tensor(out=y, in0=b, scalar=1.5, in1=y, op0=ALU.add, op1=ALU.mult))
                return y

            def residual_and_norm(b):
                ln.at(b * LN_STEPS)
                dve.wait_ge(proj_mm, b + 1)
                ln(dve.tensor_tensor(xs[:, :], ps_proj, bp_bc[:, :], ALU.add))
                dve.wait_ge(xb_in, b * 16 + 16)
                dve.tensor_tensor(x1[:, :], xs[:, :], xin[:, :], ALU.add).then_inc(x1_ready, 1)
                dve.wait_ge(x1_ready, b + 1)
                ln(dve.bn_stats(st6[:, :], x1[:, :]), wait_apart)
                ln(dve.bn_aggr(mv[:, :], st6[:, :]))
                y = rsqrt_of(mv[:, 1:2])
                dve.tensor_scalar(xs[:, :], x1[:, :], mv[:, 0:1], y, ALU.subtract, ALU.mult).then_inc(u_ready, 1)

            def second_norm(b):
                ln.at(b * LN_STEPS + 3 + RSQRT_STEPS)
                dve.wait_ge(u_ready, b + 1)
                ln(dve.bn_stats(st6[:, :], xs[:, :]), wait_apart)
                ln(dve.bn_aggr(mv[:, :], st6[:, :]))
                y = rsqrt_of(mv[:, 1:2])
                dve.wait_ge(zT_mm, b)
                dve.tensor_scalar(xn[:, :], xs[:, :], mv[:, 0:1], y, ALU.subtract, ALU.mult).then_inc(z_ready, 1)

            ROUTER_STEPS = 8
            route = Links(dve, router_links)

            def router(b):
                route.at(b * ROUTER_STEPS)
                dve.wait_ge(lg_mm, b + 1)
                route(dve.tensor_tensor(lg[:, :], ps_lg, br_bc[:, :], ALU.add), wait_apart)
                route(dve.max(mx8[:, :], lg[:, :]))
                dve.tensor_tensor(dlt[:, 0:1], mx8[:, 0:1], mx8[:, 1:2], ALU.subtract).then_inc(delta_ready, 1)
                route(dve.max_index(mi8[:, :], mx8[:, :], lg[:, :]))
                route(dve.tensor_copy(mif[:, :], mi8[:, 0:2]))
                dve.wait_ge(tanh_ready, b + 1)
                route(dve.tensor_scalar(wtop[:, 0:1], dlt[:, 1:2], 0.5, 0.5, ALU.mult, ALU.add))
                route(dve.tensor_scalar(wtop[:, 1:2], dlt[:, 1:2], -0.5, 0.5, ALU.mult, ALU.add))
                for k in range(2):
                    route(dve.tensor_scalar(wsel[:, k], iota_f[:, 0:NE], mif[:, k:k + 1], wtop[:, k:k + 1],
                                            ALU.is_equal, ALU.mult))
                dve.wait_ge(wT_mm, b)
                dve.tensor_tensor(wf[:, 0:NE], wsel[:, 0], wsel[:, 1], ALU.add).then_inc(wf_ready, 1)
                dve.wait_ge(wf_ready, b + 1)

            def add_expert(b, e):
                u = b * (NE // 2) + e // 2
                dve.wait_ge(y_mm[e % 2], u + 1)
                if e == 0:
                    dve.wait_ge(out_stored, b * 16)
                elif e == 1:
                    dve.wait_ge(b2_added, b + 1)
                elif e % 2 == 0:
                    dve.wait_ge(y_added[1], u)
                else:
                    dve.wait_ge(y_added[0], u + 1)
                dve.scalar_tensor_tensor(out=yacc[:, :], in0=ps_y[e % 2], scalar=wf[:, e:e + 1],
                                         in1=(x1 if e == 0 else yacc)[:, :], op0=ALU.mult,
                                         op1=ALU.add).then_inc(y_added[e % 2], 1)

            def add_b2(b):
                dve.wait_ge(b2_mm, b + 1)
                dve.wait_ge(y_added[0], b * (NE // 2) + 1)
                dve.tensor_tensor(yacc[:, :], yacc[:, :], ps_b2, ALU.add).then_inc(b2_added, 1)

            def block_slot(s, prep, experts):
                if prep is not None and s == 2:
                    residual_and_norm(prep)
                if prep is not None and s == 3:
                    second_norm(prep)
                if experts is not None:
                    if s == 0:
                        router(experts)
                        add_expert(experts, 0)
                    else:
                        if s == 1:
                            add_b2(experts)
                        add_expert(experts, 2 * s - 1)
                        add_expert(experts, 2 * s)
                        if s == 3:
                            add_expert(experts, 7)

            def fast_matrix(it, s):
                scatter_matrix(1, it, s, it, base_col(it, s), False, tiles(w_sb, it, s))

            def layer2_iteration(it, groups, prep=None, experts=None, after=True):
                for s in range(GPI):
                    if s < groups and (s + 1 < groups or after):
                        fast_matrix(it + (s + 1) // GPI, (s + 1) % GPI)
                    block_slot(s, prep, experts)
                    if s < groups:
                        add_sums(1, s, it, group_base(it, s))

            def slow_pass_start(k):
                def start(w):
                    dve.wait_ge(window_moved[k], w + 1)
                    dve.tensor_scalar(wbase[:, :], wbase[:, :], float(WIN), None, ALU.add).then_inc(window_moved[k], 1)
                    wait_apart(dve, window_moved[k], w + 2)
                return start

            def slow_layer(L):
                dve.memset(wbase[:, :], -float(WIN)).then_inc(window_moved[1 + L], 1)

                def groups(it, n, w):
                    base = w * WIN
                    for s in range(GPI):
                        scatter_matrix(L, it, s, n, wbase[:, 0:1], True, nrm8[:, :], base)
                        add_sums(L, s, n, base)
                all_windows(dve, groups, slow_pass_start(1 + L))

            dve.wait_ge(w_in, 16)
            dve.wait_ge(consts_in, 16 * N_CONSTS)
            bad = flag(dve)
            with dve.If(bad < 1):
                degrees(True)
                def layer1_groups(it, groups=GPI):
                    for s in range(groups):
                        base = group_base(it, s)
                        scatter_matrix(0, it, s, it, base_col(it, s), True, tiles(w_sb, it, s), base)
                        add_sums(0, s, it, base)
                with dve.Fori(0, FULL) as it:
                    layer1_groups(it)
                layer1_groups(FULL, REM)
                dve.wait_ge(p_zeroed, NB)
                dve.memset(agg[:, :, NB * P:AW], 0.0)
                fast_matrix(0, 0)
                with dve.Fori(0, LAG_PREP) as it:
                    layer2_iteration(it, GPI)
                layer2_iteration(LAG_PREP, GPI, 0)
                with dve.Fori(LAG_EXP, FULL) as it:
                    layer2_iteration(it, GPI, it - LAG_PREP, it - LAG_EXP)
                for it in range(FULL, NB + LAG_EXP):
                    prep = it - LAG_PREP if it - LAG_PREP < NB else None
                    layer2_iteration(it, REM if it == FULL else 0, prep, it - LAG_EXP, after=False)
            with dve.Else():
                degrees(False)
                dve.memset(wbase[:, :], -float(WIN)).then_inc(window_moved[0], 1)

                def degree_windows(it, n, w):
                    for s in range(GPI):
                        window_one_hot(it, s, n, wbase[:, 0:1])
                        add_degrees(s, n, w * WIN)
                all_windows(dve, degree_windows, slow_pass_start(0))
                slow_layer(0)
                dve.wait_ge(p_zeroed, NB)
                dve.memset(agg[:, :, NB * P:AW], 0.0)
                slow_layer(1)
                with dve.Fori(0, NB) as b:
                    for s in range(GPI):
                        block_slot(s, b, None)
                    for s in range(GPI):
                        block_slot(s, None, b)

        @block.scalar
        def _(act):
            def weigh(it, s):
                act.wait_ge(hi_ready, it * GPI + s + 1)
                act.wait_ge(deg_mm[s % 2], it * 2 + s // 2)
                act.copy(wst[:, s % 2], tiles(w_sb, it, s)).then_inc(wst_ready, 1)
                act.wait_ge(wst_ready, it * GPI + s + 1)
                for j in range(TG):
                    last = act.activation(whi[:, s % 2, j], oh_hi[:, s % 2, j], ACT.Copy, scale=wst[:, s % 2, j:j + 1])
                last.then_inc(whi_ready, 1)

            def degree_iteration(it, features):
                for s in range(GPI):
                    weigh(it, s)
                    if features and s == 1:
                        act.wait_ge(f_mv, it + 1)
                        act.activation(sd1[:, :], mv[:, 1:2], ACT.Sqrt, bias=eps[:, 1:2]).then_inc(f_std, 1)
                if features:
                    act.wait_ge(f_T, it + 1)
                    act.wait_ge(f_mm, it)
                    act.copy(xT[:], ps_xT).then_inc(f_xT, 1)
                    act.wait_ge(f_mm, it + 1)
                    act.wait_ge(f_stored, it * 16)
                    act.copy(feat[:, :], ps_feat).then_inc(f_feat, 1)

            def roots(L, n, s):
                act.wait_ge(prod_ready[L], n * GPI + s + 1)
                act.activation(sd8[:, :], t8[:, :], ACT.Sqrt, bias=eps[:, 0:1]).then_inc(root_ready[L], 1)

            def node_features(b, L, adds, bias):
                for sem_, k in adds:
                    act.wait_ge(sem_, k)
                act.wait_ge((p_mm, proj_mm)[L], b)
                for k in range(KD):
                    last = act.activation(hT[:, k], agg[:, k, bass.ds(b * P, P)], ACT.Relu, bias=bias[:, k:k + 1])
                last.then_inc((p_h, h7_ready)[L], 1)

            def layer1_block_a(b, adds):
                node_features(b, 0, adds, b6c)
                wait_apart(act, p_h, b + 1)
                act.copy(agg[:, :, bass.ds(b * P, P)], zero[:, :].rearrange("p (k n) -> p k n", k=KD)
                         ).then_inc(p_zeroed, 1)

            def layer1_block_b(b):
                act.wait_ge(p_mm, b + 1)
                act.wait_ge(p_stored, b * 16)
                act.copy(feat[:, :], ps_proj).then_inc(p_out, 1)

            def fast_adds(L, it, groups=GPI):
                if groups:
                    return [(added[L][0], it * 2 + 1)]
                return [(added[L][i], len(range(i, NG, 2))) for i in range(2)]

            def layer1_iteration(it, groups, b=None):
                for s in range(GPI):
                    if s < groups:
                        roots(0, it, s)
                    if b is not None and s == 0:
                        layer1_block_a(b, fast_adds(0, it, groups))
                    if b is not None and s == 2:
                        layer1_block_b(b)

            def gelu(b, e):
                u = b * (NE // 2) + e // 2
                act.wait_ge(h_mm[e % 2], u + 1)
                act.wait_ge(y_mm[e % 2], u)
                for c in range(HC):
                    last = act.activation(hs[:, e % 2, c], ps_h[e % 2][:, c], ACT.Gelu,
                                          bias=b1c[:, e * HC + c:e * HC + c + 1])
                last.then_inc(gelu_done[e % 2], 1)

            def block_slot(s, prep, adds, experts):
                if experts is not None and s == 0:
                    gelu(experts, 0)
                    act.wait_ge(delta_ready, experts + 1)
                    act.activation(dlt[:, 1:2], dlt[:, 0:1], ACT.Tanh, scale=0.5).then_inc(tanh_ready, 1)
                    gelu(experts, 1)
                    act.wait_ge(wT_mm, experts + 1)
                    act.wait_ge(b2_mm, experts)
                    act.copy(wT[0:NE, :], ps_wT[0:NE, :]).then_inc(wT_ready, 1)
                if prep is not None and s == 1:
                    node_features(prep, 1, adds, b7c)
                if experts is not None and s > 0:
                    gelu(experts, 2 * s)
                    gelu(experts, 2 * s + 1)
                if prep is not None and s == 3:
                    act.wait_ge(zT_mm, prep + 1)
                    for k in range(KD):
                        last = act.activation(xT[:, k], ps_zT[:, k], ACT.Identity, bias=bec[:, k:k + 1],
                                              scale=gac[:, k:k + 1])
                    last.then_inc(zT_ready, 1)

            def layer2_iteration(it, groups, prep=None, experts=None):
                for s in range(GPI):
                    block_slot(s, prep, fast_adds(1, it, groups), experts)

            act.wait_ge(w_in, 16)
            act.wait_ge(consts_in, 16 * N_CONSTS)
            bad = flag(act)
            with act.Fori(0, NB) as it:
                degree_iteration(it, True)
            with act.Fori(NB, NIT) as it:
                degree_iteration(it, False)
            with act.If(bad < 1):
                with act.Fori(0, LAG_PREP) as it:
                    layer1_iteration(it, GPI)
                with act.Fori(LAG_PREP, FULL) as it:
                    layer1_iteration(it, GPI, it - LAG_PREP)
                for it in range(FULL, NB + LAG_PREP):
                    layer1_iteration(it, REM if it == FULL else 0, it - LAG_PREP)
                layer2_iteration(LAG_PREP, GPI, 0)
                with act.Fori(LAG_EXP, FULL) as it:
                    layer2_iteration(it, GPI, it - LAG_PREP, it - LAG_EXP)
                for it in range(FULL, NB + LAG_EXP):
                    prep = it - LAG_PREP if it - LAG_PREP < NB else None
                    layer2_iteration(it, REM if it == FULL else 0, prep, it - LAG_EXP)
            with act.Else():
                def window_weights(it, n, w):
                    for s in range(GPI):
                        act.wait_ge(win_mm[s % 2], n * 2 + s // 2)
                        act.copy(wst[:, s % 2], tiles(w_sb, it, s)).then_inc(wwst_ready, 1)
                all_windows(act, window_weights)
                all_windows(act, lambda it, n, w: [roots(0, n, s) for s in range(GPI)])
                done = [[(added[L][i], SLOW_ITS * 2) for i in range(2)] for L in range(2)]
                with act.Fori(0, NB) as b:
                    layer1_block_a(b, done[0])
                    layer1_block_b(b)
                all_windows(act, lambda it, n, w: [roots(1, n, s) for s in range(GPI)])
                with act.Fori(0, NB) as b:
                    for s in range(GPI):
                        block_slot(s, b, done[1], None)
                    for s in range(GPI):
                        block_slot(s, None, None, b)

        @block.tensor
        def _(pe):
            def out_degrees(it, s):
                pe.wait_ge(lo_ready, it * GPI + s + 1)
                pe.wait_ge(whi_ready, it * GPI + s + 1)
                for j in range(TG):
                    last = pe.matmul(ps_do, oh_lo[:, s % 2, j], whi[:, s % 2, j], start=False, stop=False)
                last.then_inc(deg_mm[s % 2], 1)

            def in_degrees(s, n, weights_ready):
                pe.wait_ge(weights_ready, n * GPI + s + 1)
                pe.wait_ge(win_ready, n * GPI + s + 1)
                pe.wait_ge(di_added[s % 2], n * 2 + s // 2)
                for j in range(TG):
                    last = pe.matmul(ps_win[s % 2], wst[:, s % 2, j:j + 1].broadcast_to([P, P]), oh_win[:, s % 2, j],
                                     start=(j == 0), stop=(j == TG - 1))
                last.then_inc(win_mm[s % 2], 1)

            def degree_iteration(it, fast, features):
                for s in range(GPI):
                    if fast:
                        in_degrees(s, it, wst_ready)
                    out_degrees(it, s)
                    if features and s == 2:
                        pe.wait_ge(f_norm, it + 1)
                        pe.wait_ge(f_xT, it)
                        for k in range(KD):
                            last = pe.transpose(ps_xT[:, k], xn[:, k * P:(k + 1) * P], ident[:, :])
                        last.then_inc(f_T, 1)
                if features:
                    pe.wait_ge(f_xT, it + 1)
                    pe.wait_ge(f_feat, it)
                    for k in range(KD):
                        last = pe.matmul(ps_feat, xT[:, k], w6[:, k], start=(k == 0), stop=(k == KD - 1))
                    last.then_inc(f_mm, 1)

            def degrees(fast):
                with pe.Fori(0, NB) as it:
                    degree_iteration(it, fast, True)
                with pe.Fori(NB, NIT) as it:
                    degree_iteration(it, fast, False)
                pe.matmul(ps_do, ident[:, :], zero[:, 0:NB], start=False, stop=True).then_inc(do_closed, 1)

            def sums(L, s, n):
                pe.wait_ge(gathered[L][s], n * (16 * TG) + 16 * TG)
                pe.wait_ge(s_ready[L], n * GPI + s + 1)
                pe.wait_ge(added[L][s % 2], n * 2 + s // 2)
                for k in range(KD):
                    for j in range(TG):
                        last = pe.matmul(ps_seg[s % 2][:, k], gat[:, s, j, k * P:(k + 1) * P], s_mat[:, s, j],
                                         start=(j == 0), stop=(j == TG - 1))
                last.then_inc(seg_done[L][s], 1)

            def project(b, L, weights):
                pe.wait_ge((p_h, h7_ready)[L], b + 1)
                pe.wait_ge((p_out, x1_ready)[L], b)
                for k in range(KD):
                    last = pe.matmul(ps_proj, hT[:, k], weights[:, k], start=(k == 0), stop=(k == KD - 1))
                last.then_inc((p_mm, proj_mm)[L], 1)

            def layer1_iteration(it, groups, b=None):
                for s in range(GPI):
                    if s < groups:
                        sums(0, s, it)
                    if b is not None and s == 1:
                        project(b, 0, w7)

            def expert_up(b, e):
                u = b * (NE // 2) + e // 2
                pe.wait_ge(gelu_done[e % 2], u)
                for c in range(HC):
                    for k in range(KD):
                        last = pe.matmul(ps_h[e % 2][:, c], w1_sb[:, e, k, c * P:(c + 1) * P], xT[:, k],
                                         start=(k == 0), stop=(k == KD - 1))
                last.then_inc(h_mm[e % 2], 1)

            def expert_down(b, e):
                u = b * (NE // 2) + e // 2
                pe.wait_ge(gelu_done[e % 2], u + 1)
                pe.wait_ge(y_added[e % 2], u)
                for c in range(HC):
                    last = pe.matmul(ps_y[e % 2], hs[:, e % 2, c], w2_sb[:, e, c], start=(c == 0), stop=(c == HC - 1))
                last.then_inc(y_mm[e % 2], 1)

            def block_slot(s, prep, experts):
                if experts is not None and s == 0:
                    pe.wait_ge(zT_ready, experts + 1)
                    pe.wait_ge(wT_ready, experts)
                    pe.wait_ge(b2_added, experts)
                    for k in range(KD):
                        last = pe.matmul(ps_lg, xT[:, k], wr[:, k], start=(k == 0), stop=(k == KD - 1))
                    last.then_inc(lg_mm, 1)
                    expert_up(experts, 0)
                    expert_up(experts, 1)
                    expert_down(experts, 0)
                    pe.wait_ge(wf_ready, experts + 1)
                    pe.transpose(ps_wT, wf[:, :], ident[:, :]).then_inc(wT_mm, 1)
                if experts is not None and s > 0:
                    if s == 1:
                        pe.wait_ge(wT_ready, experts + 1)
                        pe.matmul(ps_b2, wT[0:NE, :], b2s[:, :], start=True, stop=True).then_inc(b2_mm, 1)
                    for e in (2 * s, 2 * s + 1):
                        expert_up(experts, e)
                        if e < NE - 1:
                            expert_down(experts, e - 1)
                if prep is not None and s == 1:
                    project(prep, 1, wp)
                if prep is not None and s == 3:
                    pe.wait_ge(z_ready, prep + 1)
                    pe.wait_ge(zT_ready, prep)
                    for k in range(KD):
                        last = pe.transpose(ps_zT[:, k], xn[:, k * P:(k + 1) * P], ident[:, :])
                    last.then_inc(zT_mm, 1)
                if experts is not None and s == 3:
                    expert_down(experts, NE - 2)
                    expert_down(experts, NE - 1)

            def layer2_iteration(it, groups, prep=None, experts=None):
                for s in range(GPI):
                    if s < groups:
                        sums(1, s, it)
                    block_slot(s, prep, experts)

            pe.wait_ge(consts_in, 16 * N_CONSTS)
            bad = flag(pe)
            pe.matmul(ps_do, ident[:, :], zero[:, 0:NB], start=True, stop=False)
            with pe.If(bad < 1):
                degrees(True)
                with pe.Fori(0, LAG_PREP) as it:
                    layer1_iteration(it, GPI)
                with pe.Fori(LAG_PREP, FULL) as it:
                    layer1_iteration(it, GPI, it - LAG_PREP)
                for it in range(FULL, NB + LAG_PREP):
                    layer1_iteration(it, REM if it == FULL else 0, it - LAG_PREP)
                pe.wait_ge(w1_in, 16)
                pe.wait_ge(w2_in, 16)
                with pe.Fori(0, LAG_PREP) as it:
                    layer2_iteration(it, GPI)
                layer2_iteration(LAG_PREP, GPI, 0)
                with pe.Fori(LAG_EXP, FULL) as it:
                    layer2_iteration(it, GPI, it - LAG_PREP, it - LAG_EXP)
                for it in range(FULL, NB + LAG_EXP):
                    prep = it - LAG_PREP if it - LAG_PREP < NB else None
                    layer2_iteration(it, REM if it == FULL else 0, prep, it - LAG_EXP)
            with pe.Else():
                degrees(False)
                all_windows(pe, lambda it, n, w: [in_degrees(s, n, wwst_ready) for s in range(GPI)])
                all_windows(pe, lambda it, n, w: [sums(0, s, n) for s in range(GPI)])
                with pe.Fori(0, NB) as b:
                    project(b, 0, w7)
                all_windows(pe, lambda it, n, w: [sums(1, s, n) for s in range(GPI)])
                pe.wait_ge(w1_in, 16)
                pe.wait_ge(w2_in, 16)
                with pe.Fori(0, NB) as b:
                    for s in range(GPI):
                        block_slot(s, b, None)
                    for s in range(GPI):
                        block_slot(s, None, b)


def kernel(**inputs):
    import numpy as np
    import concourse.bacc as bacc
    from concourse.bass_utils import run_bass_kernel_spmd

    a = {k: np.ascontiguousarray(v) for k, v in inputs.items()}
    n, d = a["x"].shape
    e = a["src"].shape[0]
    ne, _, h = a["L0_ffn_W1"].shape
    n_groups = ceil_div(e, P * TG)
    padded = ceil_div(n_groups, GPI) * GPI * P * TG
    rows = ceil_div(n, P) * P

    def by_partition(v, fill):
        full = np.full(padded, fill, v.dtype)
        full[:e] = v
        return np.ascontiguousarray(full.reshape(-1, P, TG).transpose(1, 0, 2).reshape(P, -1))

    def by_column(v):
        return np.ascontiguousarray(v.reshape(-1, P).T)

    xp = np.zeros((rows, d), a["x"].dtype)
    xp[:n] = a["x"]
    arrays = {
        "x": xp,
        "src": by_partition(a["src"], 0),
        "dst": by_partition(a["dst"], n - 1),
        "edge_weight": by_partition(a["edge_weight"], 0),
        "W6": a["L0_gnn_W6"], "W7": a["L0_gnn_W7"], "Wp": a["L0_gnn_Wp"], "Wr": a["L0_ffn_Wr"],
        "b6": by_column(a["L0_gnn_b6"]), "b7": by_column(a["L0_gnn_b7"]),
        "bp": a["L0_gnn_bp"].reshape(1, d), "br": a["L0_ffn_br"].reshape(1, ne),
        "gamma": by_column(a["L0_ffn_gamma"]), "beta": by_column(a["L0_ffn_beta"]),
        "b1": by_column(a["L0_ffn_b1"]), "b2": a["L0_ffn_b2"],
        "W1": np.ascontiguousarray(a["L0_ffn_W1"].reshape(ne, d // P, P, h).transpose(2, 0, 1, 3).reshape(P, -1)),
        "W2": np.ascontiguousarray(a["L0_ffn_W2"].reshape(ne, h // P, P, d).transpose(2, 0, 1, 3).reshape(P, -1)),
    }
    nc = bacc.Bacc("TRN2", target_bir_lowering=False, num_devices=1)
    aps = {k: nc.dram_tensor(f"in_{k}", v.shape, mybir.dt.from_np(v.dtype), kind="ExternalInput").ap()
           for k, v in arrays.items()}
    aps["out"] = nc.dram_tensor("out_y", (n, d), F32, kind="ExternalOutput").ap()
    aps.update(n_nodes=n, n_groups=n_groups, n_experts=ne, hidden=h)
    gnn_moe_kernel(nc, aps)
    r = run_bass_kernel_spmd(nc, [{f"in_{k}": v for k, v in arrays.items()}], core_ids=[0])
    return r.results[0]["out_y"]
```

```python
from contextlib import ExitStack

import concourse.bass as bass
from concourse import mybir

F32 = mybir.dt.float32
BF16 = mybir.dt.bfloat16
I32 = mybir.dt.int32
U32 = mybir.dt.uint32
ALU = mybir.AluOpType
ACT = mybir.ActivationFunctionType
AX_X = mybir.AxisListType.X
RMAX = bass.bass_isa.ReduceOp.max

P = 128
TG = 8
WIN = 64
GPI = 8
RING = 4
PT = 2
AHEAD = 2
LAG_PREP = 2
LAG_EXP = 3
NEWTON = 3
RSQRT_MAGIC = 0x5F3759DF


def ceil_div(a, b):
    return -(-a // b)


class Links:

    def __init__(self, eng, sem):
        self.eng, self.sem, self.base, self.n = eng, sem, 0, 0

    def at(self, base):
        self.base, self.n = base, 0
        return self

    def __call__(self, ins, wait=None):
        self.n += 1
        ins.then_inc(self.sem, 1)
        if wait:
            wait(self.eng, self.sem, self.base + self.n)
        else:
            self.eng.wait_ge(self.sem, self.base + self.n)


def gnn_moe_kernel(nc, A):
    x, src, dst, ew = A["x"], A["src"], A["dst"], A["edge_weight"]
    out = A["out"]
    N, D = A["n_nodes"], x.shape[1]
    E8 = src.shape[1]
    NG = A["n_groups"]
    NE = A["n_experts"]
    H = A["hidden"]
    KD = D // P
    HC = H // P
    NIT = E8 // (TG * GPI)
    FULL, REM = NG // GPI, NG % GPI
    NPAIR = ceil_div(N, PT * P)
    NB = NPAIR * PT
    NPASS = NB * P // WIN
    AW = NB * P + WIN
    ROW = D + 1
    LAST = N - (NPAIR - 1) * PT * P
    assert KD == 2 and D == 256 and NE == 8 and HC == 4 and REM >= AHEAD
    assert FULL > LAG_EXP and NPAIR == FULL and NIT == FULL + 1 and 0 < LAST <= P
    EXPERT_W = NE * KD * H
    HALF = GPI // 2
    TURNS = GPI // RING

    with ExitStack() as ctx:
        def sb(name, shape, dt=F32):
            return ctx.enter_context(nc.sbuf_tensor(name, shape, dt))

        def sem(name):
            return ctx.enter_context(nc.semaphore(name))

        def sems(name, n):
            return [sem(f"{name}{i}") for i in range(n)]

        table = [nc.dram_tensor(f"table{i}", (NB * P, ROW), F32, kind="Internal").ap() for i in range(2)]

        w_sb = sb("w_sb", [P, E8])
        dst_f = sb("dst_f", [P, E8])
        agg = sb("agg", [P, KD, AW])
        w1_di = sb("w1_di", [P, max(EXPERT_W, AW)])
        w2_src = sb("w2_src", [P, max(NE * HC * D, 4 * E8)])
        gat = sb("gat", [P, RING, TG, ROW])
        idx = sb("idx", [P, RING, TG], I32)
        s_mat = sb("s_mat", [P, RING, TG, WIN])
        oh_win = sb("oh_win", [P, RING, TG, WIN], BF16)
        di_bc = w1_di[:, 0:AW]
        w1_sb = w1_di[:, 0:EXPERT_W].rearrange("p (e k h) -> p e k h", e=NE, k=KD)
        w2_sb = w2_src[:, 0:NE * HC * D].rearrange("p (e c n) -> p e c n", e=NE, c=HC)
        src_i = w2_src[:, 0:E8].bitcast(I32)
        dst_i = w2_src[:, E8:2 * E8].bitcast(I32)
        src_hi_i = w2_src[:, 2 * E8:3 * E8].bitcast(I32)
        src_lo_i = w2_src[:, 3 * E8:4 * E8].bitcast(I32)
        src_hi = w2_src[:, 0:E8]
        src_lo = w2_src[:, E8:2 * E8]
        w3 = w2_src[:, 2 * E8:2 * E8 + 3 * E8 // 2].bitcast(BF16).rearrange("p (a e) -> p a e", a=3)
        gflat = gat[:].rearrange("p a b c -> p (a b c)")
        oh_lo = gflat[:, 0:2 * TG * P].rearrange("p (a t n) -> p a t n", a=2, t=TG)
        oh_hi = gflat[:, 2 * TG * P:2 * TG * (P + NB)].rearrange("p (a t n) -> p a t n", a=2, t=TG)
        o2 = 2 * TG * (P + NB)
        whi = gflat[:, o2:o2 + 2 * TG * NB].rearrange("p (a t n) -> p a t n", a=2, t=TG)
        wst3 = sb("wst3", [P, 2, 3, TG], BF16)

        iota_f = sb("iota_f", [P, P])
        row_i = sb("row_i", [P, 1], I32)
        row_f = sb("row_f", [P, 1])
        ident = sb("ident", [P, P])
        G = NIT * GPI
        scratch = s_mat[:].rearrange("p a b c -> p (a b c)")
        need_i = scratch[:, 0:G].bitcast(I32)
        need_f = scratch[:, G:2 * G]
        ends = scratch[:, 2 * G:4 * G].rearrange("p (a g) -> p a g", a=2)
        ends_all = scratch[:, 4 * G:6 * G].rearrange("p (a g) -> p a g", a=2)
        viol = scratch[:, 6 * G:9 * G].rearrange("p (a g) -> p a g", a=3)
        base_f = sb("base_f", [P, G])
        base_i = sb("base_i", [P, G], I32)
        bad_f = sb("bad_f", [P, 4])
        bad_i = sb("bad_i", [P, 1], I32)
        wbase = sb("wbase", [P, 1])
        eps = sb("eps", [P, 1])
        do_row = sb("do_row", [P, P])
        do_col = sb("do_col", [P, NB])

        wp = sb("wp", [P, KD, D])
        wr = sb("wr", [P, KD, NE])
        cols = sb("cols", [P, 4 * KD + NE * HC])
        b6c, b7c, gac, bec = (cols[:, KD * i:KD * (i + 1)] for i in range(4))
        b1c = cols[:, 4 * KD:]
        b2s = sb("b2s", [NE, D])
        br_bc = sb("br_bc", [P, NE])
        bp_bc = sb("bp_bc", [P, D])

        xin = sb("xin", [P, PT, D])
        st6 = sb("st6", [P, PT, 6])
        mv = sb("mv", [P, PT, 2])
        xn = sb("xn", [P, PT, D])
        xT = sb("xT", [P, KD, PT * P])
        feat = sb("feat", [P, PT, D])
        hT = sb("hT", [P, KD, PT * P])
        zero = sb("zero", [P, 1])

        rel = sb("rel", [P, RING, TG])
        di8 = sb("di8", [P, TG])
        t8 = sb("t8", [P, TG])
        sd8 = sb("sd8", [P, TG])
        r8 = sb("r8", [P, TG])
        nrm8 = sb("nrm8", [P, TG])
        zs = sb("zs", [WIN, 2, D])

        x1 = sb("x1", [P, PT, D])
        xs = sb("xs", [P, PT, D])
        rv = sb("rv", [P, 4, PT])
        rvi = sb("rvi", [P, PT], I32)
        lg = sb("lg", [P, PT, NE])
        mx8 = sb("mx8", [P, PT, 8])
        mi8 = sb("mi8", [P, PT, 8], U32)
        mif = sb("mif", [P, PT, 2])
        dlt = sb("dlt", [P, 2, PT])
        wtop = sb("wtop", [P, PT, 2])
        wsel = sb("wsel", [P, PT, 2, NE])
        wf = sb("wf", [P, PT, NE])
        wT = sb("wT", [NE, PT, P])
        acts = sb("acts", [P, 2 * HC * PT * P])
        w6 = acts[:, 0:KD * D].rearrange("p (k n) -> p k n", k=KD)
        w7 = acts[:, KD * D:2 * KD * D].rearrange("p (k n) -> p k n", k=KD)
        prod = acts[:, 2 * KD * D:2 * KD * D + TG * WIN].rearrange("p (t n) -> p t n", t=TG)
        hs = acts[:, :].rearrange("p (a c n) -> p a c n", a=2, c=HC)
        yacc = feat
        iota_i = xs[:, 0, 0:P].bitcast(I32)

        bank = [ctx.enter_context(nc.psum_tensor(f"bank{i}", [P, 512], F32)) for i in range(8)]

        def split(ap, a):
            return ap.rearrange("p (a n) -> p a n", a=a)

        ps_seg = [[bank[i][0:WIN, 0:D] for i in (0, 1)], [bank[0][0:WIN, 0:D]] * 2]
        ps_segT = [[split(bank[i][:, 0:KD * WIN], KD) for i in (2, 3)], [split(bank[1][:, 0:KD * WIN], KD)] * 2]
        ps_win = [bank[i][:, 0:WIN] for i in (4, 5)]
        ps_do = bank[2][0:NB, 0:P]
        ps_doT = bank[3][:, 0:P]
        ps_xT = split(bank[4][:, :], KD)
        ps_feat = split(bank[5][:, :], PT)
        ps_h = [split(bank[2 + i][:, :], HC // 2) for i in range(2)]
        ps_y = [split(bank[4 + i][:, :], PT) for i in range(2)]
        ps_proj = split(bank[6][:, :], PT)
        ps_zT = split(bank[6][:, :], KD)
        ps_lg = split(bank[7][:, 0:PT * NE], PT)
        ps_wT = split(bank[7][0:NE, P:(1 + PT) * P], PT)

        edges_in, w_in, consts_in = sem("edges_in"), sem("w_in"), sem("consts_in")
        iota_made, dve_setup = sem("iota_made"), sem("dve_setup")
        ends_made, ends_shared = sem("ends_made"), sem("ends_shared")
        setup_done = sem("setup_done")
        lo_ready, hi_ready, whi_ready = sem("lo_ready"), sem("hi_ready"), sem("whi_ready")
        deg_mm = sems("deg_mm", 2)
        do_closed, do_copied, do_turned, do_made, do_in_tables = (
            sem(n) for n in ("do_closed", "do_copied", "do_turned", "do_made", "do_in_tables"))
        x_in, f_norm, f_links, f_T, f_xT, f_mm, f_feat, f_stored = (
            sem(n) for n in ("x_in", "f_norm", "f_links", "f_T", "f_xT", "f_mm", "f_feat", "f_stored"))
        wst_ready, win_mm, di_added = sem("wst_ready"), sems("win_mm", 2), sems("di_added", 2)
        rel_ready, oh_ready = sems("rel_ready", 3), sems("oh_ready", 3)
        idx_in = [sems(f"idx_in{L}_", RING) for L in range(2)]
        gathered = [sems(f"gathered{L}_", RING) for L in range(2)]
        seg_done = [sems(f"seg_done{L}_", RING) for L in range(2)]
        seg_links = sems("seg_links", 2)
        prod_ready, root_ready = sems("prod_ready", 2), sems("root_ready", 2)
        s_ready = sems("s_ready", 2)
        z_copied = [sems(f"z_copied{L}_", 2) for L in range(2)]
        seg_turned = [sems(f"seg_turned{L}_", 2) for L in range(2)]
        added = [sems(f"added{L}_", 2) for L in range(2)]
        window_moved = sems("window_moved", 3)
        p_h, p_zeroed, p_mm, p_out, p_stored = (sem(n) for n in ("p_h", "p_zeroed", "p_mm", "p_out", "p_stored"))
        w1_in, w2_in, xb_in = sem("w1_in"), sem("w2_in"), sem("xb_in")
        h7_ready, proj_mm, ln_links, x1_ready, u_ready, z_ready, zT_mm, zT_ready = (
            sem(n) for n in ("h7_ready", "proj_mm", "ln_links", "x1_ready", "u_ready", "z_ready", "zT_mm", "zT_ready"))
        lg_mm, router_links, delta_ready, tanh_ready, wf_ready, wT_mm, wT_ready = (
            sem(n) for n in ("lg_mm", "router_links", "delta_ready", "tanh_ready", "wf_ready", "wT_mm", "wT_ready"))
        h_mm, gelu_done, y_mm, y_added = (sems(n, 2) for n in ("h_mm", "gelu_done", "y_mm", "y_added"))
        out_stored = sem("out_stored")

        N_CONSTS = 12
        SETUP_DONE = 3

        block = ctx.enter_context(nc.Block())

        def bc_mid(ap, n):
            return ap.unsqueeze(1).broadcast_to([P, n, ap.shape[-1]])

        def bc_in(ap, n):
            return ap.unsqueeze(2).broadcast_to([P, ap.shape[-1], n])

        def tiles(ap, it, s):
            return ap[:, bass.ds(it * (GPI * TG) + s * TG, TG)]

        def pair_rows(t, b):
            return t[bass.ds(b * (PT * P), PT * P), :].rearrange("(t p) n -> p t n", p=P)

        def turn(n, s):
            return n * HALF + s // 2

        def add_before(n, s):
            return (1, n * HALF + s // 2) if s % 2 == 0 else (0, n * HALF + (s + 1) // 2)

        def behind(it, s, k):
            return it + (s + k) // GPI, (s + k) % GPI

        def wait_apart(eng, sem_, value):
            if not isinstance(value, int):
                eng.compute_val(value)
            eng.wait_ge(setup_done, SETUP_DONE)
            eng.wait_ge(sem_, value)

        def flag(eng):
            eng.wait_ge(setup_done, SETUP_DONE)
            return eng.value_load(bad_i[0:1, 0:1], min_val=0, max_val=1)

        def all_windows(eng, f, before_pass=None):
            with eng.Fori(0, NPASS) as w:
                if before_pass:
                    before_pass(w)
                with eng.Fori(0, NIT) as it:
                    f(it, w * NIT + it, w)

        SLOW_ITS = NPASS * NIT
        ALL_ADDED = [[(added[L][i], len(range(i, NG, 2))) for i in range(2)] for L in range(2)]
        SLOW_ADDED = [[(added[L][i], SLOW_ITS * HALF) for i in range(2)] for L in range(2)]

        def fast_adds(L, it, groups):
            return [(added[L][0], it * HALF + 1)] if groups else ALL_ADDED[L]

        EVEN, ODD = NE // 2 + 1, NE // 2

        def y_turn(p, e):
            return p * (ODD if e % 2 else EVEN) + e // 2

        @block.sync
        def _(sp):
            sp.dma_start(src_i, src).then_inc(edges_in, 16)
            sp.dma_start(dst_i, dst).then_inc(edges_in, 16)
            sp.dma_start(w_sb[:, :], ew).then_inc(w_in, 16)
            for t, a in ((w6, A["W6"]), (w7, A["W7"]), (wp[:], A["Wp"]), (wr[:], A["Wr"])):
                sp.dma_start(t, a.rearrange("(k p) n -> p k n", p=P)).then_inc(consts_in, 16)
            for t, a in ((b6c, A["b6"]), (b7c, A["b7"]), (gac, A["gamma"]), (bec, A["beta"]), (b1c, A["b1"]),
                         (b2s[:, :], A["b2"]),
                         (br_bc[:, :], A["br"].broadcast_to([P, NE])), (bp_bc[:, :], A["bp"].broadcast_to([P, D]))):
                sp.dma_start(t, a).then_inc(consts_in, 16)

            def load_features(b):
                sp.wait_ge(f_norm, b)
                sp.dma_start(xin[:], pair_rows(x, b)).then_inc(x_in, 16)

            def store_features(b):
                sp.wait_ge(f_feat, b + 1)
                sp.dma_start(pair_rows(table[0][:, 0:D], b), feat[:]).then_inc(f_stored, 16)

            def features():
                load_features(0)
                with sp.Fori(0, NPAIR - 1) as b:
                    load_features(b + 1)
                    store_features(b)
                store_features(NPAIR - 1)
                sp.wait_ge(do_made, 1)
                for t in table:
                    sp.dma_start(t[:, D:ROW].rearrange("(b p) a -> p (b a)", p=P), do_col[:, :],
                                 allow_slow_non_contiguous=True).then_inc(do_in_tables, 16)

            def index(L, it, n, s):
                r, use = s % RING, n * TURNS + s // RING
                sp.wait_ge(gathered[L][r], use * (16 * TG))
                sp.dma_start(idx[:, r, :], tiles(src, it, s)).then_inc(idx_in[L][r], 16)

            def indices(L, it, n, groups=range(GPI)):
                for s in groups:
                    index(L, it, n, s)

            def store_table(b):
                sp.wait_ge(p_out, b + 1)
                sp.dma_start(pair_rows(table[1][:, 0:D], b), feat[:]).then_inc(p_stored, 16)

            def load_x(b):
                sp.wait_ge(x1_ready, b)
                sp.dma_start(xin[:], pair_rows(x, b)).then_inc(xb_in, 16)

            def store_out(b):
                sp.wait_ge(y_added[0], b * EVEN + EVEN)
                if isinstance(b, int) and b == NPAIR - 1:
                    sp.dma_start(out[b * PT * P:N, :], yacc[0:LAST, 0, :]).then_inc(out_stored, 16)
                else:
                    sp.dma_start(pair_rows(out, b), yacc[:]).then_inc(out_stored, 16)

            def load_experts():
                sp.dma_start(w1_sb, A["W1"].rearrange("p (e k h) -> p e k h", e=NE, k=KD)).then_inc(w1_in, 16)
                sp.dma_start(w2_sb, A["W2"].rearrange("p (e c n) -> p e c n", e=NE, c=HC)).then_inc(w2_in, 16)

            bad = flag(sp)
            features()
            with sp.If(bad < 1):
                with sp.Fori(0, LAG_PREP) as it:
                    indices(0, it, it)
                with sp.Fori(LAG_PREP, FULL) as it:
                    indices(0, it, it)
                    store_table(it - LAG_PREP)
                indices(0, FULL, FULL, range(REM))
                for b in range(FULL - LAG_PREP, NPAIR):
                    store_table(b)
                sp.wait_ge(s_ready[0], NG)
                load_experts()
                with sp.Fori(0, LAG_PREP) as it:
                    indices(1, it, it)
                for it in range(LAG_PREP, LAG_EXP + 1):
                    load_x(it - LAG_PREP)
                    indices(1, it, it)
                with sp.Fori(LAG_EXP + 1, FULL) as it:
                    load_x(it - LAG_PREP)
                    indices(1, it, it, range(RING))
                    store_out(it - LAG_EXP - 1)
                    indices(1, it, it, range(RING, GPI))
                for it in range(FULL, NPAIR + LAG_EXP + 1):
                    if it - LAG_PREP < NPAIR:
                        load_x(it - LAG_PREP)
                    if it == FULL:
                        indices(1, it, it, range(REM))
                    store_out(it - LAG_EXP - 1)
            with sp.Else():
                all_windows(sp, lambda it, n, w: indices(0, it, n))
                with sp.Fori(0, NPAIR) as b:
                    store_table(b)
                all_windows(sp, lambda it, n, w: indices(1, it, n))
                sp.wait_ge(s_ready[1], SLOW_ITS * GPI)
                load_experts()
                with sp.Fori(0, NPAIR - 1) as b:
                    load_x(b)
                    store_out(b)
                load_x(NPAIR - 1)
                store_out(NPAIR - 1)
            sp.wait_ge(out_stored, 16 * NPAIR)

        @block.gpsimd
        def _(pool):
            pool.iota(iota_i, pattern=[[1, P]], base=0, channel_multiplier=0).then_inc(iota_made, 1)
            pool.iota(row_i[:, :], pattern=[[0, 1]], base=0, channel_multiplier=1).then_inc(iota_made, 1)
            pool.iota(need_i, pattern=[[PT * P, NIT], [0, GPI]], base=-(LAG_PREP - 1) * PT * P,
                      channel_multiplier=0).then_inc(iota_made, 1)
            pool.wait_ge(ends_made, 2)
            pool.partition_all_reduce(ends_all.rearrange("p a g -> p (a g)"), ends.rearrange("p a g -> p (a g)"),
                                      P, RMAX).then_inc(ends_shared, 1)

            def gathers(L, n, groups=GPI):
                for s in range(groups):
                    r, use = s % RING, n * TURNS + s // RING
                    wait_apart(pool, idx_in[L][r], use * 16 + 16)
                    pool.wait_ge(seg_done[L][r], use)
                    for j in range(TG):
                        pool.indirect_dma_start(gat[:, r, j, :], None, table[L],
                                                bass.IndirectOffsetOnAxis(ap=idx[:, r, j:j + 1], axis=0)
                                                ).then_inc(gathered[L][r], 16)

            def table_ready(L):
                pool.wait_ge(do_in_tables, 32)
                pool.wait_ge((f_stored, p_stored)[L], 16 * NPAIR)

            bad = flag(pool)
            with pool.If(bad < 1):
                for L in range(2):
                    table_ready(L)
                    with pool.Fori(0, FULL) as it:
                        gathers(L, it)
                    gathers(L, FULL, REM)
            with pool.Else():
                for L in range(2):
                    table_ready(L)
                    all_windows(pool, lambda it, n, w: gathers(L, n))

        @block.vector
        def _(dve):
            step = Links(dve, dve_setup)
            dve.memset(zero[:, :], 0.0)
            dve.memset(do_row[:, :], 0.0)
            dve.memset(eps[:, :], 1e-12)
            dve.memset(di_bc, 0.0)
            dve.memset(agg[:].rearrange("p k n -> p (k n)"), 0.0)
            step(dve.memset(viol, 0.0))
            dve.wait_ge(edges_in, 32)
            step(dve.tensor_copy(dst_f[:, :], dst_i))
            step(dve.tensor_single_scalar(src_hi_i, src_i, 7, op=ALU.logical_shift_right))
            step(dve.tensor_single_scalar(src_lo_i, src_i, P - 1, op=ALU.bitwise_and))
            step(dve.tensor_copy(src_hi, src_hi_i))
            step(dve.tensor_copy(src_lo, src_lo_i))
            by_group = dst_f[:, :].rearrange("p (g t) -> p g t", t=TG)
            dve.tensor_reduce(ends[:, 0, :], by_group, AX_X, ALU.max).then_inc(ends_made, 1)
            dve.tensor_reduce(ends[:, 1, :], by_group, AX_X, ALU.min, negate=True).then_inc(ends_made, 1)
            rest = agg[:, 0, 0:E8]
            dve.wait_ge(w_in, 16)
            step(dve.tensor_copy(w3[:, 0, :], w_sb[:, :]))
            step(dve.tensor_tensor(rest, w_sb[:, :], w3[:, 0, :], ALU.subtract))
            step(dve.tensor_copy(w3[:, 1, :], rest))
            step(dve.tensor_tensor(rest, rest, w3[:, 1, :], ALU.subtract))
            step(dve.tensor_copy(w3[:, 2, :], rest))
            dve.memset(rest, 0.0).then_inc(setup_done, 1)
            dve.wait_ge(iota_made, 3)
            dve.tensor_copy(iota_f[:, :], iota_i)
            dve.tensor_copy(row_f[:, :], row_i[:, :])
            step(dve.tensor_copy(need_f, need_i))
            step(dve.tensor_scalar(ident[:, :], iota_f[:, :], row_f[:, 0:1], None, ALU.is_equal))
            dve.wait_ge(ends_shared, 1)
            step(dve.tensor_scalar(base_f[:, :], ends_all[:, 1, :], -1.0, None, ALU.mult))
            dve.tensor_copy(base_i[:, :], base_f[:, :]).then_inc(setup_done, 1)
            step(dve.tensor_tensor(viol[:, 0, :], ends_all[:, 0, :], base_f[:, :], ALU.subtract))
            step(dve.tensor_scalar(viol[:, 0, :], viol[:, 0, :], float(WIN), None, ALU.is_ge))
            step(dve.tensor_tensor(viol[:, 1, :], base_f[:, :], need_f, ALU.is_lt))
            step(dve.tensor_tensor(viol[:, 2, 0:NG - AHEAD], ends_all[:, 0, 0:NG - AHEAD], base_f[:, AHEAD:NG],
                                   ALU.is_ge))
            step(dve.tensor_reduce(bad_f[:, 0:3], viol[:, :, 0:NG], AX_X, ALU.max))
            step(dve.tensor_reduce(bad_f[:, 3:4], bad_f[:, 0:3], AX_X, ALU.max))
            dve.tensor_copy(bad_i[:, :], bad_f[:, 3:4]).then_inc(setup_done, 1)

            def rsqrt_of(link, var):
                v, y, a, b = (rv[:, i, :] for i in range(4))
                link(dve.tensor_scalar(v, var, 1e-5, None, ALU.add))
                link(dve.tensor_single_scalar(rvi[:, :], v.bitcast(I32), 1, op=ALU.logical_shift_right))
                link(dve.tensor_scalar(y.bitcast(I32), rvi[:, :], -1.0, float(RSQRT_MAGIC), ALU.mult, ALU.add))
                for _ in range(NEWTON):
                    link(dve.tensor_tensor(a, y, y, ALU.mult))
                    link(dve.tensor_tensor(b, a, v, ALU.mult))
                    link(dve.tensor_scalar(a, b, -0.5, 1.5, ALU.mult, ALU.add))
                    link(dve.tensor_tensor(y, a, y, ALU.mult))
                return y

            NORM_STEPS = 2 + 3 + 4 * NEWTON

            def norm_of(link, given):
                for t in range(PT):
                    last = dve.bn_stats(st6[:, t, :], given[:, t, :])
                link(last, wait_apart)
                for t in range(PT):
                    last = dve.bn_aggr(mv[:, t, :], st6[:, t, :])
                link(last)
                return rsqrt_of(link, mv[:, :, 1])

            def normalize(to, given, y):
                for t in range(PT):
                    last = dve.tensor_scalar(to[:, t, :], given[:, t, :], mv[:, t, 0:1], y[:, t:t + 1], ALU.subtract,
                                             ALU.mult)
                return last

            feats = Links(dve, f_links)

            def one_hots(it, s):
                dve.wait_ge(deg_mm[s % 2], turn(it, s))
                dve.tensor_tensor(oh_hi[:, s % 2], bc_mid(iota_f[:, 0:NB], TG), bc_in(tiles(src_hi, it, s), NB),
                                  ALU.is_equal).then_inc(hi_ready, 1)
                dve.tensor_tensor(oh_lo[:, s % 2], bc_mid(iota_f[:, :], TG), bc_in(tiles(src_lo, it, s), P),
                                  ALU.is_equal).then_inc(lo_ready, 1)

            def feature_norm(b):
                feats.at(b * NORM_STEPS)
                dve.wait_ge(x_in, b * 16 + 16)
                y = norm_of(feats, xin)
                dve.wait_ge(f_T, b)
                normalize(xn, xin, y).then_inc(f_norm, 1)
                dve.wait_ge(f_norm, b + 1)

            with dve.Fori(0, FULL) as it:
                for s in range(GPI):
                    one_hots(it, s)
                    if s == 1:
                        feature_norm(it)
            for s in range(REM):
                one_hots(FULL, s)
            dve.wait_ge(do_closed, 1)
            dve.tensor_copy(do_row[0:NB, :], ps_do).then_inc(do_copied, 1)
            dve.wait_ge(do_turned, 1)
            dve.tensor_copy(do_col[:, :], ps_doT[:, 0:NB]).then_inc(do_made, 1)

            def group_base(it, s):
                return dve.value_load(base_i[0:1, bass.ds(it * GPI + s, 1)], min_val=0, max_val=N - 1)

            def base_col(it, s):
                return base_f[:, bass.ds(it * GPI + s, 1)]

            def window_one_hot(phase, it, s, n, col):
                r = s % RING
                dve.tensor_scalar(rel[:, r], tiles(dst_f, it, s), col, None, ALU.subtract).then_inc(rel_ready[phase], 1)
                dve.wait_ge(rel_ready[phase], n * GPI + s + 1)
                dve.tensor_tensor(oh_win[:, r], bc_mid(iota_f[:, 0:WIN], TG), bc_in(rel[:, r], WIN),
                                  ALU.is_equal).then_inc(oh_ready[phase], 1)

            def add_degrees(n, s, base):
                dve.wait_ge(win_mm[s % 2], turn(n, s) + 1)
                par, k = add_before(n, s)
                dve.wait_ge(di_added[par], k)
                win = di_bc[:, bass.ds(base, WIN)]
                dve.tensor_tensor(win, win, ps_win[s % 2], ALU.add).then_inc(di_added[s % 2], 1)

            seg = [Links(dve, seg_links[L]) for L in range(2)]

            def edge_norms(L, it, s, n, norms, base):
                link = seg[L].at((n * GPI + s) * 4)
                r, use = s % RING, n * TURNS + s // RING
                dve.wait_ge(oh_ready[1 + L], n * GPI + s + 1)
                win = di_bc[:, bass.ds(base, WIN)]
                link(dve.tensor_tensor(prod, oh_win[:, r], bc_mid(win, TG), ALU.mult))
                link(dve.tensor_reduce(di8[:, :], prod, AX_X, ALU.add))
                dve.wait_ge(gathered[L][r], use * (16 * TG) + 16 * TG)
                dve.tensor_tensor(t8[:, :], di8[:, :], gat[:, r, :, D], ALU.mult).then_inc(prod_ready[L], 1)
                dve.wait_ge(root_ready[L], n * GPI + s + 1)
                link(dve.reciprocal(r8[:, :], sd8[:, :]))
                link(dve.tensor_tensor(norms, r8[:, :], tiles(w_sb, it, s), ALU.mult))

            def scatter_matrix(L, s, n, norms):
                r = s % RING
                dve.wait_ge(oh_ready[1 + L], n * GPI + s + 1)
                dve.tensor_tensor(s_mat[:, r], oh_win[:, r], bc_in(norms, WIN), ALU.mult).then_inc(s_ready[L], 1)

            def add_sums(L, s, n, base):
                dve.wait_ge(seg_turned[L][s % 2], turn(n, s) + 1)
                par, k = add_before(n, s)
                dve.wait_ge(added[L][par], k)
                win = agg[:, :, bass.ds(base, WIN)]
                dve.tensor_tensor(win, win, ps_segT[L][s % 2], ALU.add).then_inc(added[L][s % 2], 1)

            LN_STEPS = 1 + 2 * NORM_STEPS
            ln = Links(dve, ln_links)

            def residual_and_norm(b):
                ln.at(b * LN_STEPS)
                dve.wait_ge(proj_mm, b + 1)
                ln(dve.tensor_tensor(xs[:], ps_proj, bc_mid(bp_bc[:, :], PT), ALU.add))
                dve.wait_ge(xb_in, b * 16 + 16)
                dve.tensor_tensor(x1[:], xs[:], xin[:], ALU.add).then_inc(x1_ready, 1)
                dve.wait_ge(x1_ready, b + 1)
                normalize(xs, x1, norm_of(ln, x1)).then_inc(u_ready, 1)

            def second_norm(b):
                ln.at(b * LN_STEPS + 1 + NORM_STEPS)
                dve.wait_ge(u_ready, b + 1)
                y = norm_of(ln, xs)
                dve.wait_ge(zT_mm, b)
                normalize(xn, xs, y).then_inc(z_ready, 1)

            ROUTER_STEPS = 8
            route = Links(dve, router_links)

            def router(b):
                route.at(b * ROUTER_STEPS)
                dve.wait_ge(lg_mm, b + 1)
                route(dve.tensor_tensor(lg[:], ps_lg, bc_mid(br_bc[:, :], PT), ALU.add), wait_apart)
                for t in range(PT):
                    last = dve.max(mx8[:, t, :], lg[:, t, :])
                route(last)
                dve.tensor_tensor(dlt[:, 0, :], mx8[:, :, 0], mx8[:, :, 1], ALU.subtract).then_inc(delta_ready, 1)
                for t in range(PT):
                    last = dve.max_index(mi8[:, t, :], mx8[:, t, :], lg[:, t, :])
                route(last)
                route(dve.tensor_copy(mif[:], mi8[:, :, 0:2]))
                route(dve.tensor_tensor(wsel[:].rearrange("p t k e -> p (t k) e"), bc_mid(iota_f[:, 0:NE], 2 * PT),
                                        bc_in(mif[:].rearrange("p t k -> p (t k)"), NE), ALU.is_equal))
                dve.wait_ge(tanh_ready, b + 1)
                route(dve.tensor_scalar(wtop[:, :, 0], dlt[:, 1, :], 0.5, 0.5, ALU.mult, ALU.add))
                route(dve.tensor_scalar(wtop[:, :, 1], dlt[:, 1, :], -0.5, 0.5, ALU.mult, ALU.add))
                route(dve.tensor_tensor(wsel[:].rearrange("p t k e -> p (t k) e"),
                                        wsel[:].rearrange("p t k e -> p (t k) e"),
                                        bc_in(wtop[:].rearrange("p t k -> p (t k)"), NE), ALU.mult))
                dve.wait_ge(wT_mm, b)
                dve.tensor_tensor(wf[:], wsel[:, :, 0, :], wsel[:, :, 1, :], ALU.add).then_inc(wf_ready, 1)
                dve.wait_ge(wf_ready, b + 1)

            def add_expert(b, e, nt):
                dve.wait_ge(y_mm[e % 2], y_turn(b, e) + 1)
                if e == 0:
                    dve.wait_ge(out_stored, b * 16)
                else:
                    dve.wait_ge(y_added[(e - 1) % 2], y_turn(b, e - 1) + 1)
                for t in range(nt):
                    if e == NE:
                        last = dve.tensor_tensor(yacc[:, t, :], yacc[:, t, :], ps_y[0][:, t, :], ALU.add)
                    else:
                        last = dve.scalar_tensor_tensor(
                            out=yacc[:, t, :], in0=ps_y[e % 2][:, t, :], scalar=wf[:, t, e:e + 1],
                            in1=(x1 if e == 0 else yacc)[:, t, :], op0=ALU.mult, op1=ALU.add)
                last.then_inc(y_added[e % 2], 1)

            def pair_slot(s, prep, experts, nt=PT):
                if prep is not None and s == 2:
                    residual_and_norm(prep)
                if prep is not None and s == 3:
                    second_norm(prep)
                if experts is not None:
                    if s == 0:
                        router(experts)
                    else:
                        add_expert(experts, s - 1, nt)
                    if s == GPI - 1:
                        add_expert(experts, NE - 1, nt)
                        add_expert(experts, NE, nt)

            def next_matrix(it, s):
                window_one_hot(2, it, s, it, base_col(it, s))
                scatter_matrix(1, s, it, tiles(w_sb, it, s))

            def layer2_iteration(it, groups, prep=None, experts=None, nt=PT, after=True):
                for s in range(GPI):
                    if s < groups and (s + 1 < groups or after):
                        next_matrix(*behind(it, s, 1))
                    base = group_base(it, s) if s < groups else None
                    pair_slot(s, prep, experts, nt)
                    if s < groups:
                        add_sums(1, s, it, base)

            def degrees_ahead(it, s):
                add_degrees(it, s, group_base(it, s))

            def matrix_ahead(it, s, base, last_degrees):
                sem_, k = last_degrees
                dve.wait_ge(sem_, k)
                norms = tiles(w_sb, it, s)
                edge_norms(0, it, s, it, norms, base)
                scatter_matrix(0, s, it, norms)

            def layer1_iteration(it, groups, after=True):
                for s in range(groups):
                    if s + AHEAD + 1 < groups or after:
                        it3, s3 = behind(it, s, AHEAD + 1)
                        window_one_hot(1, it3, s3, it3, base_col(it3, s3))
                    base = group_base(it, s)
                    if s + 1 < groups or after:
                        it1, s1 = behind(it, s, 1)
                        next_base = group_base(it1, s1)
                    if s + AHEAD < groups or after:
                        it2, s2 = behind(it, s, AHEAD)
                        degrees_ahead(it2, s2)
                    if s + 1 < groups or after:
                        it2, s2 = behind(it, s, AHEAD if s + AHEAD < groups or after else 1)
                        matrix_ahead(it1, s1, next_base, (di_added[s2 % 2], turn(it2, s2) + 1))
                    add_sums(0, s, it, base)

            def pass_start(k):
                def start(w):
                    dve.wait_ge(window_moved[k], w + 1)
                    dve.tensor_scalar(wbase[:, :], wbase[:, :], float(WIN), None, ALU.add).then_inc(window_moved[k], 1)
                    wait_apart(dve, window_moved[k], w + 2)
                return start

            def slow_layer(L):
                dve.memset(wbase[:, :], -float(WIN)).then_inc(window_moved[1 + L], 1)

                def groups(it, n, w):
                    for s in range(GPI):
                        window_one_hot(1 + L, it, s, n, wbase[:, 0:1])
                        edge_norms(L, it, s, n, nrm8[:, :], w * WIN)
                        scatter_matrix(L, s, n, nrm8[:, :])
                        add_sums(L, s, n, w * WIN)
                all_windows(dve, groups, pass_start(1 + L))

            def last_columns():
                dve.wait_ge(p_zeroed, NPAIR)
                dve.memset(agg[:, :, NB * P:AW], 0.0)

            dve.wait_ge(consts_in, 16 * N_CONSTS)
            bad = flag(dve)
            with dve.If(bad < 1):
                for s in range(AHEAD + 1):
                    window_one_hot(1, 0, s, 0, base_col(0, s))
                for s in range(AHEAD):
                    degrees_ahead(0, s)
                matrix_ahead(0, 0, group_base(0, 0), (di_added[1], 1))
                with dve.Fori(0, FULL) as it:
                    layer1_iteration(it, GPI)
                layer1_iteration(FULL, REM, after=False)
                last_columns()
                next_matrix(0, 0)
                with dve.Fori(0, LAG_PREP) as it:
                    layer2_iteration(it, GPI)
                layer2_iteration(LAG_PREP, GPI, 0)
                with dve.Fori(LAG_EXP, FULL) as it:
                    layer2_iteration(it, GPI, it - LAG_PREP, it - LAG_EXP)
                for it in range(FULL, NPAIR + LAG_EXP):
                    prep = it - LAG_PREP if it - LAG_PREP < NPAIR else None
                    layer2_iteration(it, REM if it == FULL else 0, prep, it - LAG_EXP,
                                     1 if it - LAG_EXP == NPAIR - 1 else PT, after=False)
            with dve.Else():
                dve.memset(wbase[:, :], -float(WIN)).then_inc(window_moved[0], 1)

                def degree_windows(it, n, w):
                    for s in range(GPI):
                        window_one_hot(0, it, s, n, wbase[:, 0:1])
                        add_degrees(n, s, w * WIN)
                all_windows(dve, degree_windows, pass_start(0))
                slow_layer(0)
                last_columns()
                slow_layer(1)
                with dve.Fori(0, NPAIR) as b:
                    for s in range(GPI):
                        pair_slot(s, b, None)
                    for s in range(GPI):
                        pair_slot(s, None, b)

        @block.scalar
        def _(act):
            def weigh(it, s):
                act.wait_ge(hi_ready, it * GPI + s + 1)
                act.wait_ge(deg_mm[s % 2], turn(it, s))
                for j in range(TG):
                    last = act.activation(whi[:, s % 2, j], oh_hi[:, s % 2, j], ACT.Copy,
                                          scale=w_sb[:, bass.ds(it * (GPI * TG) + s * TG + j, 1)])
                last.then_inc(whi_ready, 1)

            def feature_copies(b, stage):
                if stage == 0:
                    act.wait_ge(f_T, b + 1)
                    act.wait_ge(f_mm, b)
                    act.copy(xT[:], ps_xT).then_inc(f_xT, 1)
                else:
                    act.wait_ge(f_mm, b + 1)
                    act.wait_ge(f_stored, b * 16)
                    act.copy(feat[:], ps_feat).then_inc(f_feat, 1)

            def stage_weights(it, s, n):
                act.wait_ge(win_mm[s % 2], turn(n, s))
                act.copy(wst3[:, s % 2], w3[:, :, bass.ds(it * (GPI * TG) + s * TG, TG)]).then_inc(wst_ready, 1)

            def roots(L, n, s):
                act.wait_ge(prod_ready[L], n * GPI + s + 1)
                act.activation(sd8[:, :], t8[:, :], ACT.Sqrt, bias=eps[:, 0:1]).then_inc(root_ready[L], 1)

            def copy_sums(L, n, s):
                r, use = s % RING, n * TURNS + s // RING
                act.wait_ge(seg_done[L][r], use + 1)
                act.wait_ge(seg_turned[L][s % 2], turn(n, s))
                act.copy(zs[:, s % 2], ps_seg[L][s % 2]).then_inc(z_copied[L][s % 2], 1)

            def node_features(b, L, adds, bias):
                for sem_, k in adds:
                    act.wait_ge(sem_, k)
                act.wait_ge((p_mm, proj_mm)[L], b)
                for k in range(KD):
                    last = act.activation(hT[:, k], agg[:, k, bass.ds(b * (PT * P), PT * P)], ACT.Relu,
                                          bias=bias[:, k:k + 1])
                last.then_inc((p_h, h7_ready)[L], 1)

            def layer1_pair_a(b, adds):
                node_features(b, 0, adds, b6c)
                wait_apart(act, p_h, b + 1)
                act.copy(agg[:, :, bass.ds(b * (PT * P), PT * P)], zero[:, :].unsqueeze(2).broadcast_to([P, KD, PT * P])).then_inc(p_zeroed, 1)

            def layer1_pair_b(b):
                act.wait_ge(p_mm, b + 1)
                act.wait_ge(p_stored, b * 16)
                act.copy(feat[:], ps_proj).then_inc(p_out, 1)

            def layer1_iteration(it, groups, b=None, after=True):
                for s in range(GPI):
                    if s < groups:
                        if s + AHEAD < groups or after:
                            it2, s2 = behind(it, s, AHEAD)
                            stage_weights(it2, s2, it2)
                        roots(0, it, s)
                    if b is not None and s == 1:
                        layer1_pair_a(b, fast_adds(0, it, groups))
                    if s < groups:
                        copy_sums(0, it, s)
                    if b is not None and s == 2:
                        layer1_pair_b(b)

            def gelu(b, e):
                for u in range(2):
                    act.wait_ge(h_mm[u], b * NE + e + 1)
                    act.wait_ge(y_mm[e % 2], b * (ODD if e % 2 else EVEN) + e // 2)
                    for c in range(HC // 2):
                        col = e * HC + u * (HC // 2) + c
                        last = act.activation(hs[:, e % 2, u * (HC // 2) + c], ps_h[u][:, c], ACT.Gelu,
                                              bias=b1c[:, col:col + 1])
                    last.then_inc(gelu_done[u], 1)

            def pair_slot(s, prep, adds, experts):
                if prep is not None and s == 1:
                    node_features(prep, 1, adds, b7c)
                if experts is not None:
                    if s == 0:
                        act.wait_ge(delta_ready, experts + 1)
                        act.activation(dlt[:, 1, :], dlt[:, 0, :], ACT.Tanh, scale=0.5).then_inc(tanh_ready, 1)
                    gelu(experts, s)
                    if s == 1:
                        act.wait_ge(wT_mm, experts + 1)
                        act.wait_ge(y_mm[0], experts * EVEN)
                        act.copy(wT[:], ps_wT).then_inc(wT_ready, 1)
                if prep is not None and s == GPI - 1:
                    act.wait_ge(zT_mm, prep + 1)
                    for k in range(KD):
                        last = act.activation(xT[:, k], ps_zT[:, k], ACT.Identity, bias=bec[:, k:k + 1],
                                              scale=gac[:, k:k + 1])
                    last.then_inc(zT_ready, 1)

            def layer2_iteration(it, groups, prep=None, experts=None):
                for s in range(GPI):
                    if s < groups:
                        copy_sums(1, it, s)
                    pair_slot(s, prep, fast_adds(1, it, groups), experts)

            act.wait_ge(w_in, 16)
            act.wait_ge(consts_in, 16 * N_CONSTS)
            bad = flag(act)
            with act.Fori(0, FULL) as it:
                for s in range(GPI):
                    weigh(it, s)
                    if s == 3:
                        feature_copies(it, 0)
                    if s == 5:
                        feature_copies(it, 1)
            for s in range(REM):
                weigh(FULL, s)
            with act.If(bad < 1):
                for s in range(AHEAD):
                    stage_weights(0, s, 0)
                with act.Fori(0, LAG_PREP) as it:
                    layer1_iteration(it, GPI)
                with act.Fori(LAG_PREP, FULL) as it:
                    layer1_iteration(it, GPI, it - LAG_PREP)
                for it in range(FULL, NPAIR + LAG_PREP):
                    layer1_iteration(it, REM if it == FULL else 0, it - LAG_PREP, after=False)
                with act.Fori(0, LAG_PREP) as it:
                    layer2_iteration(it, GPI)
                layer2_iteration(LAG_PREP, GPI, 0)
                with act.Fori(LAG_EXP, FULL) as it:
                    layer2_iteration(it, GPI, it - LAG_PREP, it - LAG_EXP)
                for it in range(FULL, NPAIR + LAG_EXP):
                    prep = it - LAG_PREP if it - LAG_PREP < NPAIR else None
                    layer2_iteration(it, REM if it == FULL else 0, prep, it - LAG_EXP)
            with act.Else():
                def slow_groups(L):
                    def groups(it, n, w):
                        for s in range(GPI):
                            roots(L, n, s)
                            copy_sums(L, n, s)
                    return groups
                all_windows(act, lambda it, n, w: [stage_weights(it, s, n) for s in range(GPI)])
                all_windows(act, slow_groups(0))
                with act.Fori(0, NPAIR) as b:
                    layer1_pair_a(b, SLOW_ADDED[0])
                    layer1_pair_b(b)
                all_windows(act, slow_groups(1))
                with act.Fori(0, NPAIR) as b:
                    for s in range(GPI):
                        pair_slot(s, b, SLOW_ADDED[1], None)
                    for s in range(GPI):
                        pair_slot(s, None, None, b)

        @block.tensor
        def _(pe):
            def out_degrees(it, s):
                pe.wait_ge(lo_ready, it * GPI + s + 1)
                pe.wait_ge(whi_ready, it * GPI + s + 1)
                for j in range(TG):
                    last = pe.matmul(ps_do, whi[:, s % 2, j], oh_lo[:, s % 2, j], start=False, stop=False)
                last.then_inc(deg_mm[s % 2], 1)

            def features(b, stage):
                if stage == 0:
                    pe.wait_ge(f_norm, b + 1)
                    pe.wait_ge(f_xT, b)
                    for t in range(PT):
                        for k in range(KD):
                            last = pe.transpose(ps_xT[:, k, t * P:(t + 1) * P], xn[:, t, k * P:(k + 1) * P], ident[:, :])
                    last.then_inc(f_T, 1)
                else:
                    pe.wait_ge(f_xT, b + 1)
                    pe.wait_ge(f_feat, b)
                    for t in range(PT):
                        for k in range(KD):
                            last = pe.matmul(ps_feat[:, t], xT[:, k, t * P:(t + 1) * P], w6[:, k], start=(k == 0),
                                             stop=(k == KD - 1))
                    last.then_inc(f_mm, 1)

            def in_degrees(phase, n, s):
                pe.wait_ge(wst_ready, n * GPI + s + 1)
                pe.wait_ge(oh_ready[phase], n * GPI + s + 1)
                pe.wait_ge(di_added[s % 2], turn(n, s))
                for i in range(3):
                    for j in range(TG):
                        last = pe.matmul(ps_win[s % 2], wst3[:, s % 2, i, j:j + 1].broadcast_to([P, P]),
                                         oh_win[:, s % RING, j], start=(i == 0 and j == 0),
                                         stop=(i == 2 and j == TG - 1))
                last.then_inc(win_mm[s % 2], 1)

            def sums(L, s, n):
                r, use = s % RING, n * TURNS + s // RING
                pe.wait_ge(gathered[L][r], use * (16 * TG) + 16 * TG)
                pe.wait_ge(s_ready[L], n * GPI + s + 1)
                pe.wait_ge(z_copied[L][s % 2], turn(n, s))
                for j in range(TG):
                    last = pe.matmul(ps_seg[L][s % 2], s_mat[:, r, j], gat[:, r, j, 0:D], start=(j == 0),
                                     stop=(j == TG - 1))
                last.then_inc(seg_done[L][r], 1)

            def turn_sums(L, s, n):
                wait_apart(pe, z_copied[L][s % 2], turn(n, s) + 1)
                par, k = (s % 2, turn(n, s)) if L == 0 else add_before(n, s)
                pe.wait_ge(added[L][par], k)
                for k in range(KD):
                    last = pe.transpose(ps_segT[L][s % 2][:, k], zs[:, s % 2, k * P:(k + 1) * P], ident[0:WIN, 0:WIN])
                last.then_inc(seg_turned[L][s % 2], 1)

            def project(b, L, weights):
                pe.wait_ge((p_h, h7_ready)[L], b + 1)
                pe.wait_ge((p_out, x1_ready)[L], b)
                if L == 1:
                    pe.wait_ge(zT_ready, b)
                for t in range(PT):
                    for k in range(KD):
                        last = pe.matmul(ps_proj[:, t], hT[:, k, t * P:(t + 1) * P], weights[:, k], start=(k == 0),
                                         stop=(k == KD - 1))
                last.then_inc((p_mm, proj_mm)[L], 1)

            def layer1_iteration(it, groups, b=None, after=True):
                for s in range(GPI):
                    if s < groups:
                        if s + AHEAD < groups or after:
                            in_degrees(1, *behind(it, s, AHEAD))
                        sums(0, s, it)
                        turn_sums(0, s, it)
                    if b is not None and s == 1:
                        project(b, 0, w7)

            def expert_up(b, e, nt):
                for u in range(2):
                    pe.wait_ge(gelu_done[u], b * NE + e)
                    for c in range(HC // 2):
                        col = (u * (HC // 2) + c) * P
                        for k in range(KD):
                            last = pe.matmul(ps_h[u][:, c], w1_sb[:, e, k, col:col + P], xT[:, k], start=(k == 0),
                                             stop=(k == KD - 1))
                    last.then_inc(h_mm[u], 1)

            def expert_down(b, e, nt):
                pe.wait_ge(y_added[e % 2], y_turn(b, e))
                if e == NE:
                    pe.wait_ge(wT_ready, b + 1)
                    for t in range(nt):
                        last = pe.matmul(ps_y[0][:, t], wT[:, t], b2s[:, :], start=True, stop=True)
                    last.then_inc(y_mm[0], 1)
                    return
                for u in range(2):
                    pe.wait_ge(gelu_done[u], b * NE + e + 1)
                for t in range(nt):
                    for c in range(HC):
                        last = pe.matmul(ps_y[e % 2][:, t], hs[:, e % 2, c, t * P:(t + 1) * P], w2_sb[:, e, c],
                                         start=(c == 0), stop=(c == HC - 1))
                last.then_inc(y_mm[e % 2], 1)

            def pair_slot(s, prep, experts, nt=PT):
                if experts is not None:
                    if s == 0:
                        pe.wait_ge(zT_ready, experts + 1)
                        pe.wait_ge(wT_ready, experts)
                        for t in range(PT):
                            for k in range(KD):
                                last = pe.matmul(ps_lg[:, t], xT[:, k, t * P:(t + 1) * P], wr[:, k], start=(k == 0),
                                                 stop=(k == KD - 1))
                        last.then_inc(lg_mm, 1)
                    expert_up(experts, s, nt)
                    if s == 1:
                        pe.wait_ge(wf_ready, experts + 1)
                        for t in range(PT):
                            last = pe.transpose(ps_wT[:, t], wf[:, t], ident[:, :])
                        last.then_inc(wT_mm, 1)
                    if s > 0:
                        expert_down(experts, s - 1, nt)
                if prep is not None and s == 1:
                    project(prep, 1, wp)
                if prep is not None and s == GPI - 1:
                    pe.wait_ge(z_ready, prep + 1)
                    for t in range(PT):
                        for k in range(KD):
                            last = pe.transpose(ps_zT[:, k, t * P:(t + 1) * P], xn[:, t, k * P:(k + 1) * P], ident[:, :])
                    last.then_inc(zT_mm, 1)
                if experts is not None and s == GPI - 1:
                    expert_down(experts, NE - 1, nt)
                    expert_down(experts, NE, nt)

            def layer2_iteration(it, groups, prep=None, experts=None, nt=PT):
                for s in range(GPI):
                    if s < groups:
                        sums(1, s, it)
                    pair_slot(s, prep, experts, nt)
                    if s < groups:
                        turn_sums(1, s, it)

            pe.wait_ge(consts_in, 16 * N_CONSTS)
            bad = flag(pe)
            pe.matmul(ps_do, ident[:, 0:NB], do_row[:, :], start=True, stop=False)
            with pe.Fori(0, FULL) as it:
                for s in range(GPI):
                    out_degrees(it, s)
                    if s == 2:
                        features(it, 0)
                    if s == 4:
                        features(it, 1)
            for s in range(REM):
                out_degrees(FULL, s)
            pe.matmul(ps_do, ident[:, 0:NB], do_row[:, :], start=False, stop=True).then_inc(do_closed, 1)
            pe.wait_ge(do_copied, 1)
            pe.transpose(ps_doT, do_row[:, :], ident[:, :]).then_inc(do_turned, 1)
            with pe.If(bad < 1):
                for s in range(AHEAD):
                    in_degrees(1, 0, s)
                with pe.Fori(0, LAG_PREP) as it:
                    layer1_iteration(it, GPI)
                with pe.Fori(LAG_PREP, FULL) as it:
                    layer1_iteration(it, GPI, it - LAG_PREP)
                for it in range(FULL, NPAIR + LAG_PREP):
                    layer1_iteration(it, REM if it == FULL else 0, it - LAG_PREP, after=False)
                with pe.Fori(0, LAG_PREP) as it:
                    layer2_iteration(it, GPI)
                layer2_iteration(LAG_PREP, GPI, 0)
                pe.wait_ge(w1_in, 16)
                pe.wait_ge(w2_in, 16)
                with pe.Fori(LAG_EXP, FULL) as it:
                    layer2_iteration(it, GPI, it - LAG_PREP, it - LAG_EXP)
                for it in range(FULL, NPAIR + LAG_EXP):
                    prep = it - LAG_PREP if it - LAG_PREP < NPAIR else None
                    layer2_iteration(it, REM if it == FULL else 0, prep, it - LAG_EXP,
                                     1 if it - LAG_EXP == NPAIR - 1 else PT)
            with pe.Else():
                def slow_groups(L):
                    def groups(it, n, w):
                        for s in range(GPI):
                            sums(L, s, n)
                            turn_sums(L, s, n)
                    return groups
                all_windows(pe, lambda it, n, w: [in_degrees(0, n, s) for s in range(GPI)])
                all_windows(pe, slow_groups(0))
                with pe.Fori(0, NPAIR) as b:
                    project(b, 0, w7)
                all_windows(pe, slow_groups(1))
                pe.wait_ge(w1_in, 16)
                pe.wait_ge(w2_in, 16)
                with pe.Fori(0, NPAIR) as b:
                    for s in range(GPI):
                        pair_slot(s, b, None)
                    for s in range(GPI):
                        pair_slot(s, None, b)


def kernel(**inputs):
    import numpy as np
    import concourse.bacc as bacc
    from concourse.bass_utils import run_bass_kernel_spmd

    a = {k: np.ascontiguousarray(v) for k, v in inputs.items()}
    n, d = a["x"].shape
    e = a["src"].shape[0]
    ne, _, h = a["L0_ffn_W1"].shape
    n_groups = ceil_div(e, P * TG)
    padded = ceil_div(n_groups, GPI) * GPI * P * TG
    rows = ceil_div(n, PT * P) * PT * P

    def by_partition(v, fill):
        full = np.full(padded, fill, v.dtype)
        full[:e] = v
        return np.ascontiguousarray(full.reshape(-1, P, TG).transpose(1, 0, 2).reshape(P, -1))

    def by_column(v):
        return np.ascontiguousarray(v.reshape(-1, P).T)

    xp = np.zeros((rows, d), a["x"].dtype)
    xp[:n] = a["x"]
    arrays = {
        "x": xp,
        "src": by_partition(a["src"], 0),
        "dst": by_partition(a["dst"], n - 1),
        "edge_weight": by_partition(a["edge_weight"], 0),
        "W6": a["L0_gnn_W6"], "W7": a["L0_gnn_W7"], "Wp": a["L0_gnn_Wp"], "Wr": a["L0_ffn_Wr"],
        "b6": by_column(a["L0_gnn_b6"]), "b7": by_column(a["L0_gnn_b7"]),
        "bp": a["L0_gnn_bp"].reshape(1, d), "br": a["L0_ffn_br"].reshape(1, ne),
        "gamma": by_column(a["L0_ffn_gamma"]), "beta": by_column(a["L0_ffn_beta"]),
        "b1": by_column(a["L0_ffn_b1"]), "b2": a["L0_ffn_b2"],
        "W1": np.ascontiguousarray(a["L0_ffn_W1"].reshape(ne, d // P, P, h).transpose(2, 0, 1, 3).reshape(P, -1)),
        "W2": np.ascontiguousarray(a["L0_ffn_W2"].reshape(ne, h // P, P, d).transpose(2, 0, 1, 3).reshape(P, -1)),
    }
    nc = bacc.Bacc("TRN2", target_bir_lowering=False, num_devices=1)
    aps = {k: nc.dram_tensor(f"in_{k}", v.shape, mybir.dt.from_np(v.dtype), kind="ExternalInput").ap()
           for k, v in arrays.items()}
    aps["out"] = nc.dram_tensor("out_y", (n, d), F32, kind="ExternalOutput").ap()
    aps.update(n_nodes=n, n_groups=n_groups, n_experts=ne, hidden=h)
    gnn_moe_kernel(nc, aps)
    r = run_bass_kernel_spmd(nc, [{f"in_{k}": v for k, v in arrays.items()}], core_ids=[0])
    return r.results[0]["out_y"]
```

```python
from contextlib import ExitStack

import concourse.bass as bass
from concourse import mybir

F32 = mybir.dt.float32
BF16 = mybir.dt.bfloat16
I32 = mybir.dt.int32
U32 = mybir.dt.uint32
ALU = mybir.AluOpType
ACT = mybir.ActivationFunctionType
AX_X = mybir.AxisListType.X
RMAX = bass.bass_isa.ReduceOp.max

P = 128
TG = 8
TS = 4
WIN = 32
GPI = 8
RING = 4
X_LOADS = 5
PT = 2
AHEAD = 2
LAG_PREP = 2
EXP_SLOT = 3
ACT_TILES = 2
NEWTON = 3
RSQRT_MAGIC = 0x5F3759DF


def ceil_div(a, b):
    return -(-a // b)


class Links:

    def __init__(self, eng, sem):
        self.eng, self.sem, self.base, self.n = eng, sem, 0, 0

    def at(self, base):
        self.base, self.n = base, 0
        return self

    def __call__(self, ins, wait=None):
        self.n += 1
        ins.then_inc(self.sem, 1)
        if wait:
            wait(self.eng, self.sem, self.base + self.n)
        else:
            self.eng.wait_ge(self.sem, self.base + self.n)


def gnn_moe_kernel(nc, A):
    x, src, dst, ew = A["x"], A["src"], A["dst"], A["edge_weight"]
    out = A["out"]
    N, D = A["n_nodes"], x.shape[1]
    E8 = src.shape[1]
    NG = A["n_groups"]
    NE = A["n_experts"]
    H = A["hidden"]
    KD = D // P
    HC = H // P
    NIT = E8 // (TG * GPI)
    FULL, REM = NG // GPI, NG % GPI
    NPAIR = ceil_div(N, PT * P)
    NB = NPAIR * PT
    NPASS = NB * P // WIN
    NS = NG * TG // TS
    AW = NB * P + WIN
    ROW = D + 1
    LAST = N - (NPAIR - 1) * PT * P
    assert KD == 2 and D == 256 and NE == 8 and HC == 4 and REM >= AHEAD
    assert FULL > LAG_PREP + 1 and NPAIR == FULL and NIT == FULL + 1 and 0 < LAST <= P
    EXPERT_W = NE * KD * H
    TWICE = NPAIR - (FULL - X_LOADS)
    XB = NB // X_LOADS
    assert NB % X_LOADS == 0 and 0 <= TWICE <= FULL - X_LOADS
    HALF = GPI // 2
    TURNS = GPI // RING

    with ExitStack() as ctx:
        def sb(name, shape, dt=F32):
            return ctx.enter_context(nc.sbuf_tensor(name, shape, dt))

        def sem(name):
            return ctx.enter_context(nc.semaphore(name))

        def sems(name, n):
            return [sem(f"{name}{i}") for i in range(n)]

        table = [nc.dram_tensor(f"table{i}", (NB * P, ROW), F32, kind="Internal").ap() for i in range(2)]

        w_sb = sb("w_sb", [P, E8])
        dst_f = sb("dst_f", [P, E8])
        agg = sb("agg", [P, KD, AW])
        w1_di = sb("w1_di", [P, max(EXPERT_W, AW)])
        w2_src = sb("w2_src", [P, max(NE * HC * D, 4 * E8)])
        gat = sb("gat", [P, RING, TG, ROW])
        idx = sb("idx", [P, RING, TG], I32)
        s_mat = sb("s_mat", [P, RING, TG, WIN])
        oh_win = sb("oh_win", [P, RING, TG, WIN], BF16)
        di_bc = w1_di[:, 0:AW]
        w1_sb = w1_di[:, 0:EXPERT_W].rearrange("p (e k h) -> p e k h", e=NE, k=KD)
        w2_sb = w2_src[:, 0:NE * HC * D].rearrange("p (e c n) -> p e c n", e=NE, c=HC)
        src_i = w2_src[:, 0:E8].bitcast(I32)
        dst_i = w2_src[:, E8:2 * E8].bitcast(I32)
        src_hi_i = w2_src[:, 2 * E8:3 * E8].bitcast(I32)
        src_lo_i = w2_src[:, 3 * E8:4 * E8].bitcast(I32)
        src_hi = w2_src[:, 0:E8]
        src_lo = w2_src[:, E8:2 * E8]
        w3 = w2_src[:, 2 * E8:2 * E8 + 3 * E8 // 2].bitcast(BF16).rearrange("p (a e) -> p a e", a=3)
        rest = w1_di[:, 0:2 * E8].rearrange("p (a e) -> p a e", a=2)
        gflat = gat[:].rearrange("p a b c -> p (a b c)")
        o1, o2, o3 = (RING * TG * n for n in (P, P + NB, P + 2 * NB))
        oh_lo = gflat[:, 0:o1].rearrange("p (a t n) -> p a t n", a=RING, t=TG)
        oh_hi = gflat[:, o1:o2].rearrange("p (a t n) -> p a t n", a=RING, t=TG)
        whi = gflat[:, o2:o3].rearrange("p (a t n) -> p a t n", a=RING, t=TG)
        x_all = agg[:].rearrange("p k n -> p (k n)")[:, 0:NB * D].rearrange("p (b n) -> p b n", b=NB)
        wst3 = sb("wst3", [P, 2, 3, TG], BF16)

        iota_f = sb("iota_f", [P, P])
        row_i = sb("row_i", [P, 1], I32)
        row_f = sb("row_f", [P, 1])
        ident = sb("ident", [P, P])
        G = E8 // TS
        scratch = gflat
        need_i = scratch[:, 0:G].bitcast(I32)
        need_f = scratch[:, G:2 * G]
        ends = scratch[:, 2 * G:4 * G].rearrange("p (a g) -> p a g", a=2)
        ends_all = scratch[:, 4 * G:6 * G].rearrange("p (a g) -> p a g", a=2)
        viol = scratch[:, 6 * G:9 * G].rearrange("p (a g) -> p a g", a=3)
        base_f = sb("base_f", [P, G])
        base_i = sb("base_i", [P, G], I32)
        bad_f = sb("bad_f", [P, 4])
        bad_i = sb("bad_i", [P, 1], I32)
        wbase = sb("wbase", [P, 1])
        eps = sb("eps", [P, 1])
        do_row = sb("do_row", [P, P])
        do_col = sb("do_col", [P, NB])

        wp = sb("wp", [P, KD, D])
        wr = sb("wr", [P, KD, NE])
        cols = sb("cols", [P, 4 * KD + NE * HC])
        b6c, b7c, gac, bec = (cols[:, KD * i:KD * (i + 1)] for i in range(4))
        b1c = cols[:, 4 * KD:]
        b2s = sb("b2s", [NE, D])
        br_bc = sb("br_bc", [P, NE])
        bp_bc = sb("bp_bc", [P, D])

        xin = sb("xin", [P, PT, D])
        st6 = sb("st6", [P, XB, 6])
        mv_load = sb("mv_load", [P, XB, 2])
        mv = sb("mv", [P, NB, 2])
        xn = sb("xn", [P, PT, D])
        xT = sb("xT", [P, KD, PT * P])
        feat = sb("feat", [P, PT, D])
        hT = sb("hT", [P, KD, PT * P])
        zero = sb("zero", [P, 1])

        rel = sb("rel", [P, RING, TG])
        di8 = sb("di8", [P, TG])
        t8 = sb("t8", [P, TG])
        sd8 = sb("sd8", [P, TG])
        r8 = sb("r8", [P, TG])
        nrm8 = sb("nrm8", [P, TG])
        zs = sb("zs", [P, 2, D])

        x1 = sb("x1", [P, PT, D])
        xs = sb("xs", [P, PT, D])
        rv = sb("rv", [P, 4, NB])
        rvi = sb("rvi", [P, NB], I32)
        lg = sb("lg", [P, PT, NE])
        mx8 = sb("mx8", [P, PT, 8])
        mi8 = sb("mi8", [P, PT, 8], U32)
        mif = sb("mif", [P, PT, 2])
        dlt = sb("dlt", [P, 2, PT])
        wtop = sb("wtop", [P, PT, 2])
        wsel = sb("wsel", [P, PT, 2, NE])
        wf = sb("wf", [P, PT, NE])
        wT = sb("wT", [NE, PT, P])
        acts = sb("acts", [P, 2 * HC * PT * P])
        w6 = acts[:, 0:KD * D].rearrange("p (k n) -> p k n", k=KD)
        w7 = acts[:, KD * D:2 * KD * D].rearrange("p (k n) -> p k n", k=KD)
        prod = acts[:, 2 * KD * D:2 * KD * D + TG * WIN].rearrange("p (t n) -> p t n", t=TG)
        hs = acts[:, :].rearrange("p (a c n) -> p a c n", a=2, c=HC)
        yacc = feat
        iota_i = xs[:, 0, 0:P].bitcast(I32)

        bank = [ctx.enter_context(nc.psum_tensor(f"bank{i}", [P, 512], F32)) for i in range(8)]

        def split(ap, a):
            return ap.rearrange("p (a n) -> p a n", a=a)

        ps_seg = [[bank[i][:, 0:D] for i in (0, 1)], [bank[0][:, 0:D]] * 2]
        ps_segT = [[split(bank[i][:, 0:KD * P], KD) for i in (2, 3)], [split(bank[1][:, 0:KD * P], KD)] * 2]
        ps_win = [split(bank[i][:, 0:2 * WIN], 2) for i in (4, 5)]
        ps_do = bank[2][:, 0:P]
        ps_doT = bank[3][:, 0:P]
        ps_xT = split(bank[4][:, :], KD)
        ps_feat = split(bank[5][:, :], PT)
        ps_h = [split(bank[2 + i][:, :], HC // 2) for i in range(2)]
        ps_y = [split(bank[4 + i][:, :], PT) for i in range(2)]
        ps_proj = split(bank[6][:, :], PT)
        ps_zT = split(bank[6][:, :], KD)
        ps_lg = split(bank[7][:, 0:PT * NE], PT)
        ps_wT = split(bank[7][0:NE, P:(1 + PT) * P], PT)

        edges_in, w_in, consts_in = sem("edges_in"), sem("w_in"), sem("consts_in")
        iota_made, dve_setup = sem("iota_made"), sem("dve_setup")
        ends_made, ends_shared = sem("ends_made"), sem("ends_shared")
        setup_done, src_made = sem("setup_done"), sem("src_made")
        lo_ready, hi_ready, whi_ready = sem("lo_ready"), sem("hi_ready"), sem("whi_ready")
        squares_ready, act_lo_ready = sem("squares_ready"), sem("act_lo_ready")
        deg_mm = sems("deg_mm", RING)
        do_closed, do_copied, do_turned, do_made = (
            sem(n) for n in ("do_closed", "do_copied", "do_turned", "do_made"))
        do_in_table = sems("do_in_table", 2)
        x_in, stats_made, rows_summed, f_links = (sem(n) for n in ("x_in", "stats_made", "rows_summed", "f_links"))
        f_norm, f_T, f_xT, f_mm, f_feat, f_stored = (
            sem(n) for n in ("f_norm", "f_T", "f_xT", "f_mm", "f_feat", "f_stored"))
        part_made, rest_made, di_zeroed = sem("part_made"), sem("rest_made"), sem("di_zeroed")
        wst_ready, win_mm, di_added = sem("wst_ready"), sems("win_mm", 2), sems("di_added", 2)
        first_added = sem("first_added")
        rel_ready, oh_ready = sems("rel_ready", 3), sems("oh_ready", 3)
        idx_in = [sems(f"idx_in{L}_", RING) for L in range(2)]
        gathered = [sems(f"gathered{L}_", RING) for L in range(2)]
        seg_done = [sems(f"seg_done{L}_", RING) for L in range(2)]
        seg_links = sems("seg_links", 2)
        prod_ready, root_ready = sems("prod_ready", 2), sems("root_ready", 2)
        s_ready = sems("s_ready", 2)
        z_copied = [sems(f"z_copied{L}_", 2) for L in range(2)]
        seg_turned = [sems(f"seg_turned{L}_", 2) for L in range(2)]
        quarter_added = sems("quarter_added", 2)
        added = [sems(f"added{L}_", 2) for L in range(2)]
        window_moved = sems("window_moved", 3)
        p_h, p_zeroed, p_mm, p_out, p_stored = (sem(n) for n in ("p_h", "p_zeroed", "p_mm", "p_out", "p_stored"))
        w1_in, w2_in, xb_in = sem("w1_in"), sem("w2_in"), sem("xb_in")
        h7_ready, proj_mm, ln_links, x1_ready, u_ready, z_ready, zT_mm, zT_ready = (
            sem(n) for n in ("h7_ready", "proj_mm", "ln_links", "x1_ready", "u_ready", "z_ready", "zT_mm", "zT_ready"))
        lg_mm, router_links, delta_ready, tanh_ready, wf_ready, wT_mm, wT_ready = (
            sem(n) for n in ("lg_mm", "router_links", "delta_ready", "tanh_ready", "wf_ready", "wT_mm", "wT_ready"))
        h_mm, gelu_done, y_mm, y_added = (sems(n, 2) for n in ("h_mm", "gelu_done", "y_mm", "y_added"))
        out_stored = sem("out_stored")

        N_CONSTS = 12
        REACH = (AHEAD - 1) * TG // TS + 1
        SETUP_DONE = 2

        block = ctx.enter_context(nc.Block())

        def bc_mid(ap, n):
            return ap.unsqueeze(1).broadcast_to([P, n, ap.shape[-1]])

        def bc_in(ap, n):
            return ap.unsqueeze(2).broadcast_to([P, ap.shape[-1], n])

        def tiles(ap, it, s):
            return ap[:, bass.ds(it * (GPI * TG) + s * TG, TG)]

        def pair_rows(t, b):
            return t[bass.ds(b * (PT * P), PT * P), :].rearrange("(t p) n -> p t n", p=P)

        def turn(n, s):
            return n * HALF + s // 2

        def ring_turn(n, s):
            return n * TURNS + s // RING

        NORM_SLOT, XT_SLOT, PRODUCT_SLOT, FEAT_SLOT = (0, 3), (3, 6), (2, 5), (5, 7)

        def degree_iterations(eng, f, between=None):
            with eng.Fori(0, X_LOADS) as it:
                f(it, [])
            if between:
                between()
            with eng.Fori(X_LOADS, FULL - TWICE) as it:
                f(it, [it - X_LOADS])
            if TWICE:
                with eng.Fori(FULL - TWICE, FULL) as it:
                    first = it * 2 - (FULL - TWICE + X_LOADS)
                    f(it, [first, first + 1])

        def add_before(n, s):
            return (1, n * HALF + s // 2) if s % 2 == 0 else (0, n * HALF + (s + 1) // 2)

        def behind(it, s, k):
            return it + (s + k) // GPI, (s + k) % GPI

        def wait_apart(eng, sem_, value):
            if not isinstance(value, int):
                eng.compute_val(value)
            eng.wait_ge(setup_done, SETUP_DONE)
            eng.wait_ge(sem_, value)

        def flag(eng):
            eng.wait_ge(setup_done, SETUP_DONE)
            return eng.value_load(bad_i[0:1, 0:1], min_val=0, max_val=1)

        def all_windows(eng, f, before_pass=None):
            with eng.Fori(0, NPASS) as w:
                if before_pass:
                    before_pass(w)
                with eng.Fori(0, NIT) as it:
                    f(it, w * NIT + it, w)

        SLOW_ITS = NPASS * NIT
        ALL_ADDED = [[(added[L][i], len(range(i, NG, 2))) for i in range(2)] for L in range(2)]
        SLOW_ADDED = [[(added[L][i], SLOW_ITS * HALF) for i in range(2)] for L in range(2)]

        def fast_adds(L, it, groups):
            return [(added[L][1], it * HALF)] if groups else ALL_ADDED[L]

        def layer2_iterations(eng, f):
            with eng.Fori(0, LAG_PREP) as it:
                f(it, GPI, None, None, None)
            f(LAG_PREP, GPI, 0, None, 0)
            with eng.Fori(LAG_PREP + 1, FULL) as it:
                f(it, GPI, it - LAG_PREP, it - LAG_PREP - 1, it - LAG_PREP)
            for it in range(FULL, NPAIR + LAG_PREP + 1):
                new = it - LAG_PREP if it - LAG_PREP < NPAIR else None
                f(it, REM if it == FULL else 0, new, it - LAG_PREP - 1, new)

        def expert_step(s, old, new):
            return (new, s - EXP_SLOT) if s >= EXP_SLOT else (old, s - EXP_SLOT + GPI)

        def blocks_of(b):
            return 1 if isinstance(b, int) and b == NPAIR - 1 else PT

        EVEN, ODD = NE // 2 + 1, NE // 2

        def y_turn(p, e):
            return p * (ODD if e % 2 else EVEN) + e // 2

        @block.sync
        def _(sp):
            sp.dma_start(src_i, src).then_inc(edges_in, 16)
            sp.dma_start(dst_i, dst).then_inc(edges_in, 16)
            sp.dma_start(w_sb[:, :], ew).then_inc(w_in, 16)
            for i in range(X_LOADS):
                rows = x[i * XB * P:(i + 1) * XB * P, :].rearrange("(t p) n -> p t n", p=P)
                sp.dma_start(x_all[:, i * XB:(i + 1) * XB], rows).then_inc(x_in, 16)
            for t, a in ((w6, A["W6"]), (w7, A["W7"]), (wp[:], A["Wp"]), (wr[:], A["Wr"])):
                sp.dma_start(t, a.rearrange("(k p) n -> p k n", p=P)).then_inc(consts_in, 16)
            for t, a in ((b6c, A["b6"]), (b7c, A["b7"]), (gac, A["gamma"]), (bec, A["beta"]), (b1c, A["b1"]),
                         (b2s[:, :], A["b2"]),
                         (br_bc[:, :], A["br"].broadcast_to([P, NE])), (bp_bc[:, :], A["bp"].broadcast_to([P, D]))):
                sp.dma_start(t, a).then_inc(consts_in, 16)

            def features():
                with sp.Fori(0, NPAIR) as b:
                    sp.wait_ge(f_feat, b + 1)
                    sp.dma_start(pair_rows(table[0][:, 0:D], b), feat[:]).then_inc(f_stored, 16)
                sp.wait_ge(do_made, 1)
                for t, stored in zip(table, do_in_table):
                    sp.dma_start(t[:, D:ROW].rearrange("(b p) a -> p (b a)", p=P), do_col[:, :],
                                 allow_slow_non_contiguous=True).then_inc(stored, 16)

            def index(L, it, n, s):
                r, use = s % RING, n * TURNS + s // RING
                sp.wait_ge(gathered[L][r], use * (16 * TG))
                sp.dma_start(idx[:, r, :], tiles(src, it, s)).then_inc(idx_in[L][r], 16)

            def indices(L, it, n, groups=range(GPI)):
                for s in groups:
                    index(L, it, n, s)

            def store_table(b):
                sp.wait_ge(p_out, b + 1)
                sp.dma_start(pair_rows(table[1][:, 0:D], b), feat[:]).then_inc(p_stored, 16)

            def load_x(b):
                sp.wait_ge(x1_ready, b)
                sp.dma_start(xin[:], pair_rows(x, b)).then_inc(xb_in, 16)

            def store_out(b):
                sp.wait_ge(y_added[0], b * EVEN + EVEN)
                if isinstance(b, int) and b == NPAIR - 1:
                    sp.dma_start(out[b * PT * P:N, :], yacc[0:LAST, 0, :]).then_inc(out_stored, 16)
                else:
                    sp.dma_start(pair_rows(out, b), yacc[:]).then_inc(out_stored, 16)

            bad = flag(sp)
            features()
            with sp.If(bad < 1):
                with sp.Fori(0, LAG_PREP) as it:
                    indices(0, it, it)
                with sp.Fori(LAG_PREP, FULL) as it:
                    indices(0, it, it)
                    store_table(it - LAG_PREP)
                indices(0, FULL, FULL, range(REM))
                for b in range(FULL - LAG_PREP, NPAIR):
                    store_table(b)

                def layer2_iteration(it, groups, prep, old, new):
                    if prep is not None:
                        load_x(prep)
                    indices(1, it, it, range(groups))
                    if old is not None:
                        store_out(old)

                layer2_iterations(sp, layer2_iteration)
            with sp.Else():
                all_windows(sp, lambda it, n, w: indices(0, it, n))
                with sp.Fori(0, NPAIR) as b:
                    store_table(b)
                all_windows(sp, lambda it, n, w: indices(1, it, n))
                with sp.Fori(0, NPAIR - 1) as b:
                    load_x(b)
                    store_out(b)
                load_x(NPAIR - 1)
                store_out(NPAIR - 1)
            sp.wait_ge(out_stored, 16 * NPAIR)

        @block.gpsimd
        def _(pool):
            pool.iota(iota_i, pattern=[[1, P]], base=0, channel_multiplier=0).then_inc(iota_made, 1)
            pool.iota(row_i[:, :], pattern=[[0, 1]], base=0, channel_multiplier=1).then_inc(iota_made, 1)
            pool.iota(need_i, pattern=[[PT * P, NIT], [0, GPI * TG // TS]], base=-(LAG_PREP - 1) * PT * P,
                      channel_multiplier=0).then_inc(iota_made, 1)
            pool.wait_ge(ends_made, 2)
            pool.partition_all_reduce(ends_all.rearrange("p a g -> p (a g)"), ends.rearrange("p a g -> p (a g)"),
                                      P, RMAX).then_inc(ends_shared, 1)
            for i in range(2):
                pool.wait_ge(part_made, i + 1)
                pool.tensor_tensor(rest[:, i], w_sb[:, :] if i == 0 else rest[:, 0], w3[:, i, :],
                                   ALU.subtract).then_inc(rest_made, 1)

            def weigh(it, s):
                r = s % RING
                pool.wait_ge(hi_ready, it * GPI + s + 1)
                pool.wait_ge(deg_mm[r], ring_turn(it, s))
                pool.tensor_tensor(whi[:, r], oh_hi[:, r], bc_in(tiles(w_sb, it, s), NB),
                                   ALU.mult).then_inc(whi_ready, 1)

            def gathers(L, n, groups=GPI):
                for s in range(groups):
                    r, use = s % RING, n * TURNS + s // RING
                    wait_apart(pool, idx_in[L][r], use * 16 + 16)
                    pool.wait_ge(seg_done[L][r], use)
                    for j in range(TG):
                        pool.indirect_dma_start(gat[:, r, j, :], None, table[L],
                                                bass.IndirectOffsetOnAxis(ap=idx[:, r, j:j + 1], axis=0)
                                                ).then_inc(gathered[L][r], 16)

            def table_ready(L):
                pool.wait_ge(do_in_table[L], 16)
                pool.wait_ge((f_stored, p_stored)[L], 16 * NPAIR)

            bad = flag(pool)
            with pool.Fori(0, FULL) as it:
                for s in range(GPI):
                    weigh(it, s)
            for s in range(REM):
                weigh(FULL, s)
            with pool.If(bad < 1):
                for L in range(2):
                    table_ready(L)
                    with pool.Fori(0, FULL) as it:
                        gathers(L, it)
                    gathers(L, FULL, REM)
            with pool.Else():
                for L in range(2):
                    table_ready(L)
                    all_windows(pool, lambda it, n, w: gathers(L, n))

        @block.vector
        def _(dve):
            step = Links(dve, dve_setup)
            dve.memset(zero[:, :], 0.0)
            dve.memset(do_row[:, :], 0.0)
            dve.memset(eps[:, :], 1e-12)
            dve.memset(agg[:].rearrange("p k n -> p (k n)")[:, NB * D:], 0.0)
            step(dve.memset(viol, 0.0))
            dve.wait_ge(edges_in, 32)
            step(dve.tensor_copy(dst_f[:, :], dst_i))
            step(dve.tensor_single_scalar(src_hi_i, src_i, 7, op=ALU.logical_shift_right))
            step(dve.tensor_single_scalar(src_lo_i, src_i, P - 1, op=ALU.bitwise_and))
            dve.tensor_copy(src_hi, src_hi_i).then_inc(src_made, 1)
            dve.tensor_copy(src_lo, src_lo_i).then_inc(src_made, 1)
            dve.wait_ge(src_made, 2)
            by_part = dst_f[:, :].rearrange("p (g t) -> p g t", t=TS)
            dve.tensor_reduce(ends[:, 0, :], by_part, AX_X, ALU.max).then_inc(ends_made, 1)
            dve.tensor_reduce(ends[:, 1, :], by_part, AX_X, ALU.min, negate=True).then_inc(ends_made, 1)
            dve.wait_ge(iota_made, 3)
            dve.tensor_copy(iota_f[:, :], iota_i)
            dve.tensor_copy(row_f[:, :], row_i[:, :])
            step(dve.tensor_copy(need_f, need_i))
            step(dve.tensor_scalar(ident[:, :], iota_f[:, :], row_f[:, 0:1], None, ALU.is_equal))
            dve.wait_ge(ends_shared, 1)
            step(dve.tensor_scalar(base_f[:, :], ends_all[:, 1, :], -1.0, None, ALU.mult))
            dve.tensor_copy(base_i[:, :], base_f[:, :]).then_inc(setup_done, 1)
            step(dve.tensor_tensor(viol[:, 0, :], ends_all[:, 0, :], base_f[:, :], ALU.subtract))
            step(dve.tensor_scalar(viol[:, 0, :], viol[:, 0, :], float(WIN), None, ALU.is_ge))
            step(dve.tensor_tensor(viol[:, 1, :], base_f[:, :], need_f, ALU.is_lt))
            step(dve.tensor_tensor(viol[:, 2, 0:NS - REACH], ends_all[:, 0, 0:NS - REACH], base_f[:, REACH:NS],
                                   ALU.is_ge))
            step(dve.tensor_reduce(bad_f[:, 0:3], viol[:, :, 0:NS], AX_X, ALU.max))
            step(dve.tensor_reduce(bad_f[:, 3:4], bad_f[:, 0:3], AX_X, ALU.max))
            dve.tensor_copy(bad_i[:, :], bad_f[:, 3:4]).then_inc(setup_done, 1)
            step(dve.tensor_tensor(by_part, by_part, bc_in(base_f[:, :], TS), ALU.subtract))

            def rsqrt_of(link, var):
                v, y, a, b = (rv[:, i, 0:var.shape[-1]] for i in range(4))
                half = rvi[:, 0:var.shape[-1]]
                link(dve.tensor_scalar(v, var, 1e-5, None, ALU.add))
                link(dve.tensor_single_scalar(half, v.bitcast(I32), 1, op=ALU.logical_shift_right))
                link(dve.tensor_scalar(y.bitcast(I32), half, -1.0, float(RSQRT_MAGIC), ALU.mult, ALU.add))
                for _ in range(NEWTON):
                    link(dve.tensor_tensor(a, y, y, ALU.mult))
                    link(dve.tensor_tensor(b, a, v, ALU.mult))
                    link(dve.tensor_scalar(a, b, -0.5, 1.5, ALU.mult, ALU.add))
                    link(dve.tensor_tensor(y, a, y, ALU.mult))
                return y

            NORM_STEPS = 2 + 3 + 4 * NEWTON

            def norm_of(link, given):
                for t in range(PT):
                    last = dve.bn_stats(st6[:, t, :], given[:, t, :])
                link(last, wait_apart)
                for t in range(PT):
                    last = dve.bn_aggr(mv[:, t, :], st6[:, t, :])
                link(last)
                return rsqrt_of(link, mv[:, 0:PT, 1])

            def normalize(to, given, y):
                for t in range(PT):
                    last = dve.tensor_scalar(to[:, t, :], given[:, t, :], mv[:, t, 0:1], y[:, t:t + 1], ALU.subtract,
                                             ALU.mult)
                return last

            def one_hots(it, s):
                r = s % RING
                dve.wait_ge(deg_mm[r], ring_turn(it, s))
                dve.tensor_tensor(oh_hi[:, r], bc_mid(iota_f[:, 0:NB], TG), bc_in(tiles(src_hi, it, s), NB),
                                  ALU.is_equal).then_inc(hi_ready, 1)
                dve.tensor_tensor(oh_lo[:, r, ACT_TILES:], bc_mid(iota_f[:, :], TG - ACT_TILES),
                                  bc_in(tiles(src_lo, it, s)[:, ACT_TILES:], P), ALU.is_equal).then_inc(lo_ready, 1)

            def row_statistics(load):
                dve.wait_ge(x_in, 16 * X_LOADS)
                for t in range(XB):
                    row = x_all[:, bass.ds(load * XB + t, 1), :].rearrange("p a n -> p (a n)")
                    last = dve.bn_stats(st6[:, t, :], row)
                last.then_inc(stats_made, 1)
                wait_apart(dve, stats_made, load * 2 + 1)
                for t in range(XB):
                    last = dve.bn_aggr(mv_load[:, t, :], st6[:, t, :])
                last.then_inc(stats_made, 1)
                dve.wait_ge(stats_made, load * 2 + 2)
                dve.tensor_copy(mv[:, bass.ds(load * XB, XB), :], mv_load[:]).then_inc(rows_summed, 1)

            def feature_norm(b):
                dve.wait_ge(f_T, b)
                for t in range(PT):
                    block = bass.ds(b * PT + t, 1)
                    last = dve.tensor_scalar(xn[:, t:t + 1, :], x_all[:, block, :], mv[:, block, 0], rv[:, 1, block],
                                             ALU.subtract, ALU.mult)
                last.then_inc(f_norm, 1)

            def degree_iteration(it, pairs):
                for s in range(GPI):
                    one_hots(it, s)
                    if not pairs and s == RING:
                        row_statistics(it)
                    for i, b in enumerate(pairs):
                        if s == NORM_SLOT[i]:
                            feature_norm(b)

            def roots_of_rows():
                dve.wait_ge(rows_summed, X_LOADS)
                rsqrt_of(Links(dve, f_links), mv[:, :, 1])

            degree_iterations(dve, degree_iteration, roots_of_rows)
            for s in range(REM):
                one_hots(FULL, s)
            dve.wait_ge(do_closed, 1)
            dve.tensor_copy(do_row[:, :], ps_do).then_inc(do_copied, 1)
            dve.wait_ge(do_turned, 1)
            step(dve.tensor_copy(do_col[:, :], ps_doT[:, 0:NB]))
            dve.tensor_tensor(do_col[:, :], do_col[:, :], ps_doT[:, P // 2:P // 2 + NB], ALU.add).then_inc(do_made, 1)

            def group_base(it, s):
                return [dve.value_load(base_i[0:1, bass.ds((it * GPI + s) * 2 + h, 1)], min_val=0, max_val=N - 1)
                        for h in range(2)]

            def window_one_hot(phase, it, s, n, rel):
                r = s % RING
                dve.tensor_tensor(oh_win[:, r], bc_mid(iota_f[:, 0:WIN], TG), bc_in(rel, WIN),
                                  ALU.is_equal).then_inc(oh_ready[phase], 1)

            def own_one_hot(phase, it, s):
                window_one_hot(phase, it, s, it, tiles(dst_f, it, s))

            def pass_one_hot(phase, it, s, n):
                dve.tensor_scalar(rel[:, s % RING], tiles(dst_f, it, s), wbase[:, 0:1], None,
                                  ALU.subtract).then_inc(rel_ready[phase], 1)
                dve.wait_ge(rel_ready[phase], n * GPI + s + 1)
                window_one_hot(phase, it, s, n, rel[:, s % RING])

            def add_degrees(n, s, bases):
                dve.wait_ge(win_mm[s % 2], turn(n, s) + 1)
                par, k = add_before(n, s)
                dve.wait_ge(di_added[par], k)
                first, second = (di_bc[:, bass.ds(base, WIN)] for base in bases)
                dve.tensor_tensor(first, first, ps_win[s % 2][:, 0], ALU.add).then_inc(first_added, 1)
                dve.wait_ge(first_added, n * GPI + s + 1)
                dve.tensor_tensor(second, second, ps_win[s % 2][:, 1], ALU.add).then_inc(di_added[s % 2], 1)

            seg = [Links(dve, seg_links[L]) for L in range(2)]

            def edge_norms(L, it, s, n, norms, bases):
                link = seg[L].at((n * GPI + s) * 4)
                r, use = s % RING, n * TURNS + s // RING
                dve.wait_ge(oh_ready[1 + L], n * GPI + s + 1)
                for h, base in enumerate(bases):
                    part = slice(h * TS, (h + 1) * TS)
                    degrees = bc_mid(di_bc[:, bass.ds(base, WIN)], TS)
                    last = dve.tensor_tensor(prod[:, part], oh_win[:, r, part], degrees, ALU.mult)
                link(last)
                link(dve.tensor_reduce(di8[:, :], prod, AX_X, ALU.add))
                dve.wait_ge(gathered[L][r], use * (16 * TG) + 16 * TG)
                dve.tensor_tensor(t8[:, :], di8[:, :], gat[:, r, :, D], ALU.mult).then_inc(prod_ready[L], 1)
                dve.wait_ge(root_ready[L], n * GPI + s + 1)
                link(dve.reciprocal(r8[:, :], sd8[:, :]))
                link(dve.tensor_tensor(norms, r8[:, :], tiles(w_sb, it, s), ALU.mult))

            def scatter_matrix(L, s, n, norms):
                r = s % RING
                dve.wait_ge(oh_ready[1 + L], n * GPI + s + 1)
                dve.tensor_tensor(s_mat[:, r], oh_win[:, r], bc_in(norms, WIN), ALU.mult).then_inc(s_ready[L], 1)

            def add_sums(L, s, n, bases):
                dve.wait_ge(seg_turned[L][s % 2], turn(n, s) + 1)
                par, k = add_before(n, s)
                dve.wait_ge(added[L][par], k)
                quarters = ps_segT[L][s % 2]
                for q in range(4):
                    win = agg[:, :, bass.ds(bases[q // 2], WIN)]
                    add = dve.tensor_tensor(win, win, quarters[:, :, q * WIN:(q + 1) * WIN], ALU.add)
                    if q < 3:
                        add.then_inc(quarter_added[L], 1)
                        dve.wait_ge(quarter_added[L], (n * GPI + s) * 3 + q + 1)
                    else:
                        add.then_inc(added[L][s % 2], 1)

            LN_STEPS = 1 + 2 * NORM_STEPS
            ln = Links(dve, ln_links)

            def residual_and_norm(b):
                ln.at(b * LN_STEPS)
                dve.wait_ge(proj_mm, b + 1)
                ln(dve.tensor_tensor(xs[:], ps_proj, bc_mid(bp_bc[:, :], PT), ALU.add))
                dve.wait_ge(xb_in, b * 16 + 16)
                dve.tensor_tensor(x1[:], xs[:], xin[:], ALU.add).then_inc(x1_ready, 1)
                dve.wait_ge(x1_ready, b + 1)
                normalize(xs, x1, norm_of(ln, x1)).then_inc(u_ready, 1)

            def second_norm(b):
                ln.at(b * LN_STEPS + 1 + NORM_STEPS)
                dve.wait_ge(u_ready, b + 1)
                y = norm_of(ln, xs)
                dve.wait_ge(zT_mm, b)
                normalize(xn, xs, y).then_inc(z_ready, 1)

            ROUTER_STEPS = 8
            route = Links(dve, router_links)

            def router(b):
                route.at(b * ROUTER_STEPS)
                dve.wait_ge(lg_mm, b + 1)
                route(dve.tensor_tensor(lg[:], ps_lg, bc_mid(br_bc[:, :], PT), ALU.add), wait_apart)
                for t in range(PT):
                    last = dve.max(mx8[:, t, :], lg[:, t, :])
                route(last)
                dve.tensor_tensor(dlt[:, 0, :], mx8[:, :, 0], mx8[:, :, 1], ALU.subtract).then_inc(delta_ready, 1)
                for t in range(PT):
                    last = dve.max_index(mi8[:, t, :], mx8[:, t, :], lg[:, t, :])
                route(last)
                route(dve.tensor_copy(mif[:], mi8[:, :, 0:2]))
                route(dve.tensor_tensor(wsel[:].rearrange("p t k e -> p (t k) e"), bc_mid(iota_f[:, 0:NE], 2 * PT),
                                        bc_in(mif[:].rearrange("p t k -> p (t k)"), NE), ALU.is_equal))
                dve.wait_ge(tanh_ready, b + 1)
                route(dve.tensor_scalar(wtop[:, :, 0], dlt[:, 1, :], 0.5, 0.5, ALU.mult, ALU.add))
                route(dve.tensor_scalar(wtop[:, :, 1], dlt[:, 1, :], -0.5, 0.5, ALU.mult, ALU.add))
                route(dve.tensor_tensor(wsel[:].rearrange("p t k e -> p (t k) e"),
                                        wsel[:].rearrange("p t k e -> p (t k) e"),
                                        bc_in(wtop[:].rearrange("p t k -> p (t k)"), NE), ALU.mult))
                dve.wait_ge(wT_mm, b)
                dve.tensor_tensor(wf[:], wsel[:, :, 0, :], wsel[:, :, 1, :], ALU.add).then_inc(wf_ready, 1)
                dve.wait_ge(wf_ready, b + 1)

            def add_expert(b, e, nt):
                dve.wait_ge(y_mm[e % 2], y_turn(b, e) + 1)
                if e == 0:
                    dve.wait_ge(out_stored, b * 16)
                else:
                    dve.wait_ge(y_added[(e - 1) % 2], y_turn(b, e - 1) + 1)
                for t in range(nt):
                    if e == NE:
                        last = dve.tensor_tensor(yacc[:, t, :], yacc[:, t, :], ps_y[0][:, t, :], ALU.add)
                    else:
                        last = dve.scalar_tensor_tensor(
                            out=yacc[:, t, :], in0=ps_y[e % 2][:, t, :], scalar=wf[:, t, e:e + 1],
                            in1=(x1 if e == 0 else yacc)[:, t, :], op0=ALU.mult, op1=ALU.add)
                last.then_inc(y_added[e % 2], 1)

            def prepare(s, b):
                if s == 0:
                    residual_and_norm(b)
                if s == 1:
                    second_norm(b)

            def expert_slot(b, e):
                if e == 0:
                    router(b)
                else:
                    add_expert(b, e - 1, blocks_of(b))
                if e == NE - 1:
                    add_expert(b, NE - 1, blocks_of(b))
                    add_expert(b, NE, blocks_of(b))

            def next_matrix(it, s):
                own_one_hot(2, it, s)
                scatter_matrix(1, s, it, tiles(w_sb, it, s))

            def layer2_iteration(it, groups, prep, old, new):
                for s in range(GPI):
                    if s < groups and (s + 1 < groups or groups == GPI):
                        next_matrix(*behind(it, s, 1))
                    bases = group_base(it, s) if s < groups else None
                    b, e = expert_step(s, old, new)
                    if prep is not None and s > 0:
                        prepare(s, prep)
                    if b is not None:
                        expert_slot(b, e)
                    if s < groups:
                        add_sums(1, s, it, bases)
                    if prep is not None and s == 0:
                        prepare(s, prep)

            def degrees_ahead(it, s):
                add_degrees(it, s, group_base(it, s))

            def matrix_ahead(it, s, bases, last_degrees):
                sem_, k = last_degrees
                dve.wait_ge(sem_, k)
                norms = tiles(w_sb, it, s)
                edge_norms(0, it, s, it, norms, bases)
                scatter_matrix(0, s, it, norms)

            def layer1_iteration(it, groups, after=True):
                for s in range(groups):
                    if s + AHEAD + 1 < groups or after:
                        it3, s3 = behind(it, s, AHEAD + 1)
                        own_one_hot(1, it3, s3)
                    base = group_base(it, s)
                    if s + 1 < groups or after:
                        it1, s1 = behind(it, s, 1)
                        next_base = group_base(it1, s1)
                    if s + AHEAD < groups or after:
                        it2, s2 = behind(it, s, AHEAD)
                        degrees_ahead(it2, s2)
                    if s + 1 < groups or after:
                        it2, s2 = behind(it, s, AHEAD if s + AHEAD < groups or after else 1)
                        matrix_ahead(it1, s1, next_base, (di_added[s2 % 2], turn(it2, s2) + 1))
                    add_sums(0, s, it, base)

            def pass_start(k):
                def start(w):
                    dve.wait_ge(window_moved[k], w + 1)
                    dve.tensor_scalar(wbase[:, :], wbase[:, :], float(WIN), None, ALU.add).then_inc(window_moved[k], 1)
                    wait_apart(dve, window_moved[k], w + 2)
                return start

            def slow_layer(L):
                dve.memset(wbase[:, :], -float(WIN)).then_inc(window_moved[1 + L], 1)

                def groups(it, n, w):
                    for s in range(GPI):
                        pass_one_hot(1 + L, it, s, n)
                        edge_norms(L, it, s, n, nrm8[:, :], [w * WIN] * 2)
                        scatter_matrix(L, s, n, nrm8[:, :])
                        add_sums(L, s, n, [w * WIN] * 2)
                all_windows(dve, groups, pass_start(1 + L))

            def last_columns():
                dve.wait_ge(p_zeroed, NPAIR)
                dve.memset(agg[:, :, NB * P:AW], 0.0)

            dve.wait_ge(consts_in, 16 * N_CONSTS)
            dve.wait_ge(di_zeroed, 1)
            bad = flag(dve)
            with dve.If(bad < 1):
                for s in range(AHEAD + 1):
                    own_one_hot(1, 0, s)
                for s in range(AHEAD):
                    degrees_ahead(0, s)
                matrix_ahead(0, 0, group_base(0, 0), (di_added[1], 1))
                with dve.Fori(0, FULL) as it:
                    layer1_iteration(it, GPI)
                layer1_iteration(FULL, REM, after=False)
                last_columns()
                next_matrix(0, 0)
                layer2_iterations(dve, layer2_iteration)
            with dve.Else():
                step(dve.tensor_tensor(by_part, by_part, bc_in(base_f[:, :], TS), ALU.add))
                dve.memset(wbase[:, :], -float(WIN)).then_inc(window_moved[0], 1)

                def degree_windows(it, n, w):
                    for s in range(GPI):
                        pass_one_hot(0, it, s, n)
                        add_degrees(n, s, [w * WIN] * 2)
                all_windows(dve, degree_windows, pass_start(0))
                slow_layer(0)
                last_columns()
                slow_layer(1)
                with dve.Fori(0, NPAIR) as b:
                    for s in range(EXP_SLOT):
                        prepare(s, b)
                    for e in range(NE):
                        expert_slot(b, e)

        @block.scalar
        def _(act):
            def act_one_hots(it, s):
                r = s % RING
                act.wait_ge(deg_mm[r], ring_turn(it, s))
                for j in range(ACT_TILES):
                    last = act.activation(oh_lo[:, r, j], iota_f[:, :], ACT.Square, scale=-1.0,
                                          bias=src_lo[:, bass.ds(it * (GPI * TG) + s * TG + j, 1)])
                last.then_inc(squares_ready, 1)
                act.wait_ge(squares_ready, it * GPI + s + 1)
                act.activation(oh_lo[:, r, 0:ACT_TILES], oh_lo[:, r, 0:ACT_TILES], ACT.Relu, scale=-2.0,
                               bias=1.0).then_inc(act_lo_ready, 1)

            def feature_copies(b, stage):
                if stage == 0:
                    act.wait_ge(f_T, b + 1)
                    act.wait_ge(f_mm, b)
                    act.copy(xT[:], ps_xT).then_inc(f_xT, 1)
                    act.copy(x_all[:, bass.ds(b * PT, PT), :], zero[:, :].unsqueeze(2).broadcast_to([P, PT, D]))
                else:
                    act.wait_ge(f_mm, b + 1)
                    act.wait_ge(f_stored, b * 16)
                    act.copy(feat[:], ps_feat).then_inc(f_feat, 1)

            def stage_weights(it, s, n):
                act.wait_ge(win_mm[s % 2], turn(n, s))
                act.copy(wst3[:, s % 2], w3[:, :, bass.ds(it * (GPI * TG) + s * TG, TG)]).then_inc(wst_ready, 1)

            def roots(L, n, s):
                act.wait_ge(prod_ready[L], n * GPI + s + 1)
                act.activation(sd8[:, :], t8[:, :], ACT.Sqrt, bias=eps[:, 0:1]).then_inc(root_ready[L], 1)

            def copy_sums(L, n, s):
                r, use = s % RING, n * TURNS + s // RING
                act.wait_ge(seg_done[L][r], use + 1)
                act.wait_ge(seg_turned[L][s % 2], turn(n, s))
                act.copy(zs[:, s % 2], ps_seg[L][s % 2]).then_inc(z_copied[L][s % 2], 1)

            def node_features(b, L, adds, bias):
                for sem_, k in adds:
                    act.wait_ge(sem_, k)
                act.wait_ge((p_mm, proj_mm)[L], b)
                for k in range(KD):
                    last = act.activation(hT[:, k], agg[:, k, bass.ds(b * (PT * P), PT * P)], ACT.Relu,
                                          bias=bias[:, k:k + 1])
                last.then_inc((p_h, h7_ready)[L], 1)

            def layer1_pair_a(b, adds):
                node_features(b, 0, adds, b6c)
                wait_apart(act, p_h, b + 1)
                act.copy(agg[:, :, bass.ds(b * (PT * P), PT * P)],
                         zero[:, :].unsqueeze(2).broadcast_to([P, KD, PT * P])).then_inc(p_zeroed, 1)

            def layer1_pair_b(b):
                act.wait_ge(p_mm, b + 1)
                act.wait_ge(p_stored, b * 16)
                act.copy(feat[:], ps_proj).then_inc(p_out, 1)

            def layer1_iteration(it, groups, b=None, after=True):
                for s in range(GPI):
                    if s < groups:
                        if s + AHEAD < groups or after:
                            it2, s2 = behind(it, s, AHEAD)
                            stage_weights(it2, s2, it2)
                        roots(0, it, s)
                    if b is not None and s == 0:
                        layer1_pair_a(b, fast_adds(0, it, groups))
                    if s < groups:
                        copy_sums(0, it, s)
                    if b is not None and s == 1:
                        layer1_pair_b(b)

            def gelu(b, e):
                for u in range(2):
                    act.wait_ge(h_mm[u], b * NE + e + 1)
                    act.wait_ge(y_mm[e % 2], b * (ODD if e % 2 else EVEN) + e // 2)
                    for c in range(HC // 2):
                        col = e * HC + u * (HC // 2) + c
                        last = act.activation(hs[:, e % 2, u * (HC // 2) + c], ps_h[u][:, c], ACT.Gelu,
                                              bias=b1c[:, col:col + 1])
                    last.then_inc(gelu_done[u], 1)

            def prepare(s, b, adds):
                if s == 0:
                    node_features(b, 1, adds, b7c)
                if s == EXP_SLOT - 1:
                    act.wait_ge(zT_mm, b + 1)
                    for k in range(KD):
                        last = act.activation(xT[:, k], ps_zT[:, k], ACT.Identity, bias=bec[:, k:k + 1],
                                              scale=gac[:, k:k + 1])
                    last.then_inc(zT_ready, 1)

            def expert_slot(b, e):
                if e == 0:
                    act.wait_ge(delta_ready, b + 1)
                    act.activation(dlt[:, 1, :], dlt[:, 0, :], ACT.Tanh, scale=0.5).then_inc(tanh_ready, 1)
                gelu(b, e)
                if e == 1:
                    act.wait_ge(wT_mm, b + 1)
                    act.wait_ge(y_mm[0], b * EVEN)
                    act.copy(wT[:], ps_wT).then_inc(wT_ready, 1)

            def layer2_iteration(it, groups, prep, old, new):
                for s in range(GPI):
                    if s < groups:
                        copy_sums(1, it, s)
                    b, e = expert_step(s, old, new)
                    if prep is not None and s == 0:
                        prepare(s, prep, fast_adds(1, it, groups))
                    if b is not None:
                        expert_slot(b, e)
                    if prep is not None and s > 0:
                        prepare(s, prep, None)

            def load_experts(matrices, count):
                act.wait_ge(matrices, count)
                w1 = A["W1"].rearrange("p (e k h) -> p e k h", e=NE, k=KD)
                w2 = A["W2"].rearrange("p (e c n) -> p e c n", e=NE, c=HC)
                for e in range(NE):
                    act.dma_start(w1_sb[:, e], w1[:, e]).then_inc(w1_in, 16)
                    act.dma_start(w2_sb[:, e], w2[:, e]).then_inc(w2_in, 16)

            act.wait_ge(w_in, 16)
            act.wait_ge(src_made, 2)
            act.copy(w3[:, 0, :], w_sb[:, :]).then_inc(part_made, 1)
            for i in range(2):
                act.wait_ge(rest_made, i + 1)
                act.copy(w3[:, i + 1, :], rest[:, i]).then_inc(part_made, 1)
            act.wait_ge(part_made, 3)
            act.copy(di_bc, zero[:, :].broadcast_to([P, AW])).then_inc(di_zeroed, 1)
            act.wait_ge(consts_in, 16 * N_CONSTS)
            bad = flag(act)
            def degree_iteration(it, pairs):
                for s in range(GPI):
                    act_one_hots(it, s)
                    for i, b in enumerate(pairs):
                        if s == XT_SLOT[i]:
                            feature_copies(b, 0)
                        if s == FEAT_SLOT[i]:
                            feature_copies(b, 1)
            degree_iterations(act, degree_iteration)
            for s in range(REM):
                act_one_hots(FULL, s)
            with act.If(bad < 1):
                for s in range(AHEAD):
                    stage_weights(0, s, 0)
                with act.Fori(0, LAG_PREP) as it:
                    layer1_iteration(it, GPI)
                with act.Fori(LAG_PREP, FULL) as it:
                    layer1_iteration(it, GPI, it - LAG_PREP)
                for it in range(FULL, NPAIR + LAG_PREP):
                    layer1_iteration(it, REM if it == FULL else 0, it - LAG_PREP, after=False)
                load_experts(s_ready[0], NG)
                layer2_iterations(act, layer2_iteration)
            with act.Else():
                def slow_groups(L):
                    def groups(it, n, w):
                        for s in range(GPI):
                            roots(L, n, s)
                            copy_sums(L, n, s)
                    return groups
                all_windows(act, lambda it, n, w: [stage_weights(it, s, n) for s in range(GPI)])
                all_windows(act, slow_groups(0))
                with act.Fori(0, NPAIR) as b:
                    layer1_pair_a(b, SLOW_ADDED[0])
                    layer1_pair_b(b)
                all_windows(act, slow_groups(1))
                load_experts(s_ready[1], SLOW_ITS * GPI)
                with act.Fori(0, NPAIR) as b:
                    for s in range(EXP_SLOT):
                        prepare(s, b, SLOW_ADDED[1])
                    for e in range(NE):
                        expert_slot(b, e)

        @block.tensor
        def _(pe):
            def out_degrees(it, s):
                pe.wait_ge(lo_ready, it * GPI + s + 1)
                pe.wait_ge(act_lo_ready, it * GPI + s + 1)
                pe.wait_ge(whi_ready, it * GPI + s + 1)
                r = s % RING
                for j in range(TG):
                    half = j % 2 * (P // 2)
                    last = pe.matmul(ps_do[half:half + NB, :], whi[:, r, j], oh_lo[:, r, j], start=False, stop=False)
                last.then_inc(deg_mm[r], 1)

            def features(b, stage):
                if stage == 0:
                    pe.wait_ge(f_norm, b + 1)
                    pe.wait_ge(f_xT, b)
                    for t in range(PT):
                        for k in range(KD):
                            last = pe.transpose(ps_xT[:, k, t * P:(t + 1) * P], xn[:, t, k * P:(k + 1) * P],
                                                ident[:, :])
                    last.then_inc(f_T, 1)
                else:
                    pe.wait_ge(f_xT, b + 1)
                    pe.wait_ge(f_feat, b)
                    for t in range(PT):
                        for k in range(KD):
                            last = pe.matmul(ps_feat[:, t], xT[:, k, t * P:(t + 1) * P], w6[:, k], start=(k == 0),
                                             stop=(k == KD - 1))
                    last.then_inc(f_mm, 1)

            def in_degrees(phase, n, s):
                pe.wait_ge(wst_ready, n * GPI + s + 1)
                pe.wait_ge(oh_ready[phase], n * GPI + s + 1)
                pe.wait_ge(di_added[s % 2], turn(n, s))
                for h in range(2):
                    for i in range(3):
                        for j in range(TS):
                            t = h * TS + j
                            part = wst3[:, s % 2, i, t:t + 1].broadcast_to([P, P])
                            last = pe.matmul(ps_win[s % 2][:, h], part, oh_win[:, s % RING, t],
                                             start=(i == 0 and j == 0), stop=(i == 2 and j == TS - 1))
                last.then_inc(win_mm[s % 2], 1)

            def sums(L, s, n):
                r, use = s % RING, n * TURNS + s // RING
                pe.wait_ge(gathered[L][r], use * (16 * TG) + 16 * TG)
                pe.wait_ge(s_ready[L], n * GPI + s + 1)
                pe.wait_ge(z_copied[L][s % 2], turn(n, s))
                for j in range(0, TS, 2):
                    for q in range(4):
                        tile = q // 2 * TS + j + q % 2
                        last = pe.matmul(ps_seg[L][s % 2][q * WIN:(q + 1) * WIN, :], s_mat[:, r, tile],
                                         gat[:, r, tile, 0:D], start=(j == 0), stop=(j == TS - 2))
                last.then_inc(seg_done[L][r], 1)

            def turn_sums(L, s, n):
                wait_apart(pe, z_copied[L][s % 2], turn(n, s) + 1)
                par, k = (s % 2, turn(n, s)) if L == 0 else add_before(n, s)
                pe.wait_ge(added[L][par], k)
                for k in range(KD):
                    last = pe.transpose(ps_segT[L][s % 2][:, k], zs[:, s % 2, k * P:(k + 1) * P], ident[:, :])
                last.then_inc(seg_turned[L][s % 2], 1)

            def project(b, L, weights):
                pe.wait_ge((p_h, h7_ready)[L], b + 1)
                pe.wait_ge((p_out, x1_ready)[L], b)
                if L == 1:
                    pe.wait_ge(zT_ready, b)
                for t in range(PT):
                    for k in range(KD):
                        last = pe.matmul(ps_proj[:, t], hT[:, k, t * P:(t + 1) * P], weights[:, k], start=(k == 0),
                                         stop=(k == KD - 1))
                last.then_inc((p_mm, proj_mm)[L], 1)

            def layer1_iteration(it, groups, b=None, after=True):
                for s in range(GPI):
                    if s < groups:
                        if s + AHEAD < groups or after:
                            in_degrees(1, *behind(it, s, AHEAD))
                        sums(0, s, it)
                        turn_sums(0, s, it)
                    if b is not None and s == 0:
                        project(b, 0, w7)

            def expert_up(b, e):
                for u in range(2):
                    pe.wait_ge(gelu_done[u], b * NE + e)
                    for c in range(HC // 2):
                        col = (u * (HC // 2) + c) * P
                        for k in range(KD):
                            last = pe.matmul(ps_h[u][:, c], w1_sb[:, e, k, col:col + P], xT[:, k], start=(k == 0),
                                             stop=(k == KD - 1))
                    last.then_inc(h_mm[u], 1)

            def expert_down(b, e, nt):
                pe.wait_ge(y_added[e % 2], y_turn(b, e))
                if e == NE:
                    pe.wait_ge(wT_ready, b + 1)
                    for t in range(nt):
                        last = pe.matmul(ps_y[0][:, t], wT[:, t], b2s[:, :], start=True, stop=True)
                    last.then_inc(y_mm[0], 1)
                    return
                for u in range(2):
                    pe.wait_ge(gelu_done[u], b * NE + e + 1)
                for t in range(nt):
                    for c in range(HC):
                        last = pe.matmul(ps_y[e % 2][:, t], hs[:, e % 2, c, t * P:(t + 1) * P], w2_sb[:, e, c],
                                         start=(c == 0), stop=(c == HC - 1))
                last.then_inc(y_mm[e % 2], 1)

            def prepare(s, b):
                if s == 0:
                    project(b, 1, wp)
                if s == EXP_SLOT - 1:
                    pe.wait_ge(z_ready, b + 1)
                    for t in range(PT):
                        for k in range(KD):
                            last = pe.transpose(ps_zT[:, k, t * P:(t + 1) * P], xn[:, t, k * P:(k + 1) * P],
                                                ident[:, :])
                    last.then_inc(zT_mm, 1)

            def expert_slot(b, e):
                if e == 0:
                    pe.wait_ge(zT_ready, b + 1)
                    pe.wait_ge(wT_ready, b)
                    for t in range(PT):
                        for k in range(KD):
                            last = pe.matmul(ps_lg[:, t], xT[:, k, t * P:(t + 1) * P], wr[:, k], start=(k == 0),
                                             stop=(k == KD - 1))
                    last.then_inc(lg_mm, 1)
                expert_up(b, e)
                if e == 1:
                    pe.wait_ge(wf_ready, b + 1)
                    for t in range(PT):
                        last = pe.transpose(ps_wT[:, t], wf[:, t], ident[:, :])
                    last.then_inc(wT_mm, 1)
                if e > 0:
                    expert_down(b, e - 1, blocks_of(b))

            def last_experts(b):
                expert_down(b, NE - 1, blocks_of(b))
                expert_down(b, NE, blocks_of(b))

            def layer2_iteration(it, groups, prep, old, new):
                if prep is not None and old is None:
                    pe.wait_ge(w1_in, 16 * NE)
                    pe.wait_ge(w2_in, 16 * NE)
                for s in range(GPI):
                    if s < groups:
                        sums(1, s, it)
                    b, e = expert_step(s, old, new)
                    if b is not None:
                        expert_slot(b, e)
                    if prep is not None:
                        prepare(s, prep)
                    if b is not None and e == NE - 1:
                        last_experts(b)
                    if s < groups:
                        turn_sums(1, s, it)

            pe.wait_ge(consts_in, 16 * N_CONSTS)
            bad = flag(pe)
            pe.matmul(ps_do, ident[:, :], do_row[:, :], start=True, stop=False)
            def degree_iteration(it, pairs):
                for s in range(GPI):
                    out_degrees(it, s)
                    for i, b in enumerate(pairs):
                        if s == NORM_SLOT[i]:
                            features(b, 0)
                        if s == PRODUCT_SLOT[i]:
                            features(b, 1)
            degree_iterations(pe, degree_iteration)
            for s in range(REM):
                out_degrees(FULL, s)
            pe.matmul(ps_do, ident[:, :], do_row[:, :], start=False, stop=True).then_inc(do_closed, 1)
            pe.wait_ge(do_copied, 1)
            pe.transpose(ps_doT, do_row[:, :], ident[:, :]).then_inc(do_turned, 1)
            with pe.If(bad < 1):
                for s in range(AHEAD):
                    in_degrees(1, 0, s)
                with pe.Fori(0, LAG_PREP) as it:
                    layer1_iteration(it, GPI)
                with pe.Fori(LAG_PREP, FULL) as it:
                    layer1_iteration(it, GPI, it - LAG_PREP)
                for it in range(FULL, NPAIR + LAG_PREP):
                    layer1_iteration(it, REM if it == FULL else 0, it - LAG_PREP, after=False)
                layer2_iterations(pe, layer2_iteration)
            with pe.Else():
                def slow_groups(L):
                    def groups(it, n, w):
                        for s in range(GPI):
                            sums(L, s, n)
                            turn_sums(L, s, n)
                    return groups
                all_windows(pe, lambda it, n, w: [in_degrees(0, n, s) for s in range(GPI)])
                all_windows(pe, slow_groups(0))
                with pe.Fori(0, NPAIR) as b:
                    project(b, 0, w7)
                all_windows(pe, slow_groups(1))
                pe.wait_ge(w1_in, 16 * NE)
                pe.wait_ge(w2_in, 16 * NE)
                with pe.Fori(0, NPAIR) as b:
                    for s in range(EXP_SLOT):
                        prepare(s, b)
                    for e in range(NE):
                        expert_slot(b, e)
                    last_experts(b)


def kernel(**inputs):
    import numpy as np
    import concourse.bacc as bacc
    from concourse.bass_utils import run_bass_kernel_spmd

    a = {k: np.ascontiguousarray(v) for k, v in inputs.items()}
    n, d = a["x"].shape
    e = a["src"].shape[0]
    ne, _, h = a["L0_ffn_W1"].shape
    n_groups = ceil_div(e, P * TG)
    padded = ceil_div(n_groups, GPI) * GPI * P * TG
    rows = ceil_div(n, PT * P) * PT * P

    def by_partition(v, fill):
        full = np.full(padded, fill, v.dtype)
        full[:e] = v
        return np.ascontiguousarray(full.reshape(-1, P, TS).transpose(1, 0, 2).reshape(P, -1))

    def by_column(v):
        return np.ascontiguousarray(v.reshape(-1, P).T)

    xp = np.zeros((rows, d), a["x"].dtype)
    xp[:n] = a["x"]
    arrays = {
        "x": xp,
        "src": by_partition(a["src"], 0),
        "dst": by_partition(a["dst"], n - 1),
        "edge_weight": by_partition(a["edge_weight"], 0),
        "W6": a["L0_gnn_W6"], "W7": a["L0_gnn_W7"], "Wp": a["L0_gnn_Wp"], "Wr": a["L0_ffn_Wr"],
        "b6": by_column(a["L0_gnn_b6"]), "b7": by_column(a["L0_gnn_b7"]),
        "bp": a["L0_gnn_bp"].reshape(1, d), "br": a["L0_ffn_br"].reshape(1, ne),
        "gamma": by_column(a["L0_ffn_gamma"]), "beta": by_column(a["L0_ffn_beta"]),
        "b1": by_column(a["L0_ffn_b1"]), "b2": a["L0_ffn_b2"],
        "W1": np.ascontiguousarray(a["L0_ffn_W1"].reshape(ne, d // P, P, h).transpose(2, 0, 1, 3).reshape(P, -1)),
        "W2": np.ascontiguousarray(a["L0_ffn_W2"].reshape(ne, h // P, P, d).transpose(2, 0, 1, 3).reshape(P, -1)),
    }
    nc = bacc.Bacc("TRN2", target_bir_lowering=False, num_devices=1)
    aps = {k: nc.dram_tensor(f"in_{k}", v.shape, mybir.dt.from_np(v.dtype), kind="ExternalInput").ap()
           for k, v in arrays.items()}
    aps["out"] = nc.dram_tensor("out_y", (n, d), F32, kind="ExternalOutput").ap()
    aps.update(n_nodes=n, n_groups=n_groups, n_experts=ne, hidden=h)
    gnn_moe_kernel(nc, aps)
    r = run_bass_kernel_spmd(nc, [{f"in_{k}": v for k, v in arrays.items()}], core_ids=[0])
    return r.results[0]["out_y"]
```
